# Optimizing a Trainium2 kernel written in Bass

```python
import numpy as np
import jax
import jax.numpy as jnp

def _softmax(x, axis=-1):
    return jax.nn.softmax(x, axis=axis)

def _gelu(x):
    return jax.nn.gelu(x, approximate=True)

def _silu(x):
    return jax.nn.silu(x)

def _sigmoid(x):
    return jax.nn.sigmoid(x)

def _layernorm(x, axis=-1, eps=1e-05):
    m = jnp.mean(x, axis=axis, keepdims=True)
    v = jnp.var(x, axis=axis, keepdims=True)
    return (x - m) / jnp.sqrt(v + eps)

def _scatter_add(tgt, idx, src, axis=0):
    return tgt.at[idx].add(src)

def _segment_sum(src, seg, n):
    return jax.ops.segment_sum(src, seg, n)
kernel_name = 'mk_xattn_ffn_d1_seqx_r2_e5b600'

def setup_inputs(seed: int=0):
    np.random.seed(seed)
    _w = jnp.asarray

    def _rec_inputs():
        import jax
        import jax.numpy as jnp
        _rk = jax.random.key(seed)
        x = 7.22e-05 + 1 * jax.random.normal(jax.random.fold_in(_rk, 1), (16, 224, 512), jnp.float32)
        _lenS = 224 - jax.random.randint(jax.random.fold_in(_rk, 7), (16,), 0, max(1, 224 // 4) + 1, jnp.int32)
        _lenS2 = 750 - jax.random.randint(jax.random.fold_in(_rk, 8), (16,), 0, max(1, 750 // 4) + 1, jnp.int32)
        _ctx_768P = jax.random.normal(jax.random.fold_in(_rk, 11), (16, 16, 384), jnp.float32)
        _ctx_768c = jax.random.dirichlet(jax.random.fold_in(_rk, 511), 0.3 * jnp.ones((16,), jnp.float32), (16, 750))
        _ctx_768t = jnp.einsum('bsk,bkd->bsd', _ctx_768c, _ctx_768P)
        _ctx_768t = _ctx_768t * jax.lax.rsqrt(jnp.mean(jnp.square(_ctx_768t)) + 1e-12) * 0.953939
        ctx_768 = -0.000191848 + 0.999787 * (_ctx_768t + 0.3 * jax.random.normal(jax.random.fold_in(_rk, 611), (16, 750, 384), jnp.float32))
        _validS = jnp.arange(224)[None, :] < _lenS[:, None]
        _validS2 = jnp.arange(750)[None, :] < _lenS2[:, None]
        _causal = jnp.tril(jnp.ones((224, 224), dtype=bool))
        mask_BxS2_bk0 = jnp.logical_not(jnp.broadcast_to(_validS2[:, :], (16, 750)))
        return (x, ctx_768, mask_BxS2_bk0)
    x, ctx_768, mask_BxS2_bk0 = _rec_inputs()

    def _L0_xattn_setup():
        import jax, jax.numpy as jnp
        import numpy as np
        HEADS = 8
        DIM_HEAD = 64
        QUERY_DIM = 512
        CONTEXT_DIM = 384
        INNER = HEADS * DIM_HEAD
        key = jax.random.key(seed)
        ks = jax.random.split(key, 8)
        b, n, j = (4, 1024, 1024)
        x = jax.random.normal(ks[0], (b, n, QUERY_DIM), dtype=jnp.float32)
        context = jax.random.normal(ks[1], (b, j, CONTEXT_DIM), dtype=jnp.float32)
        mask = jax.random.randint(ks[2], (b, j), 0, 2).astype(jnp.bool_)
        W_q = jax.random.normal(ks[3], (QUERY_DIM, INNER), dtype=jnp.float32) / np.sqrt(QUERY_DIM)
        W_k = jax.random.normal(ks[4], (CONTEXT_DIM, INNER), dtype=jnp.float32) / np.sqrt(CONTEXT_DIM)
        W_v = jax.random.normal(ks[5], (CONTEXT_DIM, INNER), dtype=jnp.float32) / np.sqrt(CONTEXT_DIM)
        W_o = jax.random.normal(ks[6], (INNER, QUERY_DIM), dtype=jnp.float32) / np.sqrt(INNER)
        b_o = jax.random.normal(ks[7], (QUERY_DIM,), dtype=jnp.float32) * 0.01
        return {'x': x, 'context': context, 'mask': mask, 'W_q': W_q, 'W_k': W_k, 'W_v': W_v, 'W_o': W_o, 'b_o': b_o}
    _L0_xattn_all = _L0_xattn_setup()
    _L0_xattn_in = {k: v for k, v in _L0_xattn_all.items() if k in ('W_q', 'W_k', 'W_v', 'W_o', 'b_o')}
    del _L0_xattn_all

    def _L0_ffn_setup():
        import jax, jax.numpy as jnp
        import numpy as np
        import math
        EMBED_DIM = 512
        FFN_DIM = 2048
        N_EXPERTS = 8
        TOP_K = 2
        CAP_FACTOR = 1.25
        key = jax.random.key(seed)
        k0, k1, k2, k3 = jax.random.split(key, 4)
        B, S = (4, 1024)
        x = jax.random.normal(k0, (B, S, EMBED_DIM), dtype=jnp.float32)
        Wr = jax.random.normal(k1, (EMBED_DIM, N_EXPERTS), dtype=jnp.float32) * 0.02
        W1 = jax.random.normal(k2, (N_EXPERTS, EMBED_DIM, FFN_DIM), dtype=jnp.float32) * 0.02
        W2 = jax.random.normal(k3, (N_EXPERTS, FFN_DIM, EMBED_DIM), dtype=jnp.float32) * 0.02
        return {'x': x, 'Wr': Wr, 'W1': W1, 'W2': W2}
    _L0_ffn_all = _L0_ffn_setup()
    _L0_ffn_in = {k: v for k, v in _L0_ffn_all.items() if k in ('Wr', 'W1', 'W2')}
    del _L0_ffn_all
    return {'x': x, 'ctx_768': ctx_768, 'mask_BxS2_bk0': mask_BxS2_bk0, 'L0_xattn_W_q': _L0_xattn_in['W_q'], 'L0_xattn_W_k': _L0_xattn_in['W_k'], 'L0_xattn_W_v': _L0_xattn_in['W_v'], 'L0_xattn_W_o': _L0_xattn_in['W_o'], 'L0_xattn_b_o': _L0_xattn_in['b_o'], 'L0_ffn_Wr': _L0_ffn_in['Wr'], 'L0_ffn_W1': _L0_ffn_in['W1'], 'L0_ffn_W2': _L0_ffn_in['W2']}

def reference(x, ctx_768, mask_BxS2_bk0, L0_xattn_W_q, L0_xattn_W_k, L0_xattn_W_v, L0_xattn_W_o, L0_xattn_b_o, L0_ffn_Wr, L0_ffn_W1, L0_ffn_W2):
    import jax
    import jax.numpy as jnp

    def _L0_xattn_ref(x, context, mask, W_q, W_k, W_v, W_o, b_o):
        import jax, jax.numpy as jnp
        import numpy as np
        HEADS = 8
        DIM_HEAD = 64
        QUERY_DIM = 512
        CONTEXT_DIM = 384
        INNER = HEADS * DIM_HEAD
        b, n, _ = x.shape
        j = context.shape[1]
        scale = DIM_HEAD ** (-0.5)
        q = (x @ W_q).reshape(b, n, HEADS, DIM_HEAD)
        k = (context @ W_k).reshape(b, j, HEADS, DIM_HEAD)
        v = (context @ W_v).reshape(b, j, HEADS, DIM_HEAD)
        sim = jnp.einsum('bihd,bjhd->bhij', q, k) * scale
        max_neg = -jnp.finfo(sim.dtype).max
        sim = jnp.where(mask[:, None, None, :], sim, max_neg)
        attn = jax.nn.softmax(sim, axis=-1)
        out = jnp.einsum('bhij,bjhd->bihd', attn, v).reshape(b, n, INNER)
        return out @ W_o + b_o

    def _L0_ffn_ref(x, Wr, W1, W2):
        import jax, jax.numpy as jnp
        import numpy as np
        import math
        EMBED_DIM = 512
        FFN_DIM = 2048
        N_EXPERTS = 8
        TOP_K = 2
        CAP_FACTOR = 1.25
        B, S, D = x.shape
        t = B * S
        xf = x.reshape(t, D)
        probs = jax.nn.softmax(xf.astype(jnp.float32) @ Wr, axis=-1)
        topk_probs, topk_experts = jax.lax.top_k(probs, TOP_K)
        cap = max(math.ceil(t * TOP_K * CAP_FACTOR / N_EXPERTS), 1)
        y = jnp.zeros_like(xf)
        for e in range(N_EXPERTS):
            mask = topk_experts == e
            gate = jnp.sum(jnp.where(mask, topk_probs, 0.0), axis=-1)
            has = jnp.any(mask, axis=-1)
            g_masked = jnp.where(has, gate, -jnp.inf)
            vals, idx = jax.lax.top_k(g_masked, cap)
            g = jnp.where(jnp.isfinite(vals), vals, 0.0)
            xe = xf[idx]
            h = jax.nn.relu(xe @ W1[e]) @ W2[e]
            y = y.at[idx].add(g[:, None] * h)
        return y.reshape(B, S, D)
    x = x + _L0_xattn_ref(_layernorm(x, axis=-1), ctx_768, mask_BxS2_bk0, L0_xattn_W_q, L0_xattn_W_k, L0_xattn_W_v, L0_xattn_W_o, L0_xattn_b_o)
    x = x + _L0_ffn_ref(_layernorm(x, axis=-1), L0_ffn_Wr, L0_ffn_W1, L0_ffn_W2)
    return x

_drawn_inputs = setup_inputs


def setup_inputs(seed=0):
    import zlib

    import numpy as np

    out = dict(_drawn_inputs(seed))
    spreads = {}
    factors = {'L0_xattn_b_o': 5.494}
    for name, (base, spread) in spreads.items():
        noise = np.random.default_rng([zlib.crc32(name.encode()), seed]).standard_normal(out[name].shape)
        drawn = base * np.exp(spread * noise) if base else spread * noise
        out[name] = jnp.asarray(drawn.astype(out[name].dtype))
    for name, factor in factors.items():
        out[name] = (out[name] * factor).astype(out[name].dtype)
    return out
```

```python
from contextlib import ExitStack

import concourse.bass as bass
from concourse import mybir

F32 = mybir.dt.float32
F32R = mybir.dt.float32r
I32 = mybir.dt.int32
U32 = mybir.dt.uint32
U8 = mybir.dt.uint8
ALU = mybir.AluOpType
ACT = mybir.ActivationFunctionType
AX = mybir.AxisListType

B, S, D = 16, 224, 512
SK, DC = 750, 384
H, DH = 8, 64
E, F = 8, 2048
NTOK = B * S
CAP = 1120
R = 112
NT = NTOK // R
KC = 125
NKEY = 2 * KC
DCH, CCH = D // 128, DC // 128
HP = H // 2
EPS = 1e-5
BIG = 3.4028234663852886e38
SCALE = -(DH ** -0.5)
NPAIR = B // 2
TP = 4
CAPT = (CAP + 127) // 128
BLK = 3
NBLK = CAPT // BLK
FCH = F // 128
NDUMP = CAPT * 128


def f32(ap):
    return ap.bitcast(F32)


def wait_unless_first(engine, sem, value):
    if not isinstance(value, int) or value > 0:
        engine.wait_ge(sem, value)


def held(engine, passed, sem, value):
    engine.wait_ge(sem, value)
    engine.sem_inc(passed, 1)


def preamble(nc, T, A):
    with ExitStack() as ctx:
        stage = ctx.enter_context(nc.sbuf_tensor("w_stage", [128, 14, D], F32))
        mrow = ctx.enter_context(nc.sbuf_tensor("mask_rows", [B, SK], U8))
        m01 = ctx.enter_context(nc.sbuf_tensor("mask_any", [B, 4], F32))
        flag_ps = ctx.enter_context(nc.psum_tensor("flag_ps", [128, 512], F32))
        sem = lambda n: ctx.enter_context(nc.semaphore(n))
        w_in, b_in, mask_in, zero_out = sem("w_in"), sem("b_in"), sem("mask_in"), sem("zero_out")
        hi_done, lo_done, cleared, ident_done = sem("hi_done"), sem("lo_done"), sem("cleared"), sem("ident_done")
        flag_step, flag_sum, zeroed = sem("flag_step"), sem("flag_sum"), sem("zeroed")
        parts = [("wq", A["wq"], DCH), ("wk", A["wk"], CCH), ("wv", A["wv"], CCH), ("wo", A["wo"], DCH)]
        block = ctx.enter_context(nc.Block())

        @block.sync
        def _(sp):
            sp.dma_start(mrow[:], A["mask"]).then_inc(mask_in, 16)
            at = 0
            for name, w, n in parts:
                sp.dma_start(stage[:, at:at + n, :], w.rearrange("(c p) n -> p c n", p=128)).then_inc(w_in, 16)
                at += n
            sp.dma_start(T["bias"][:], A["bo"].rearrange("(a n) -> a n", a=1).partition_broadcast(R)).then_inc(b_in, 16)
            sp.dma_start(T["wr"][:], A["wr"].rearrange("(c p) n -> p c n", p=128)).then_inc(b_in, 16)
            sp.wait_ge(zeroed, 1)
            for a in range(CAPT):
                sp.dma_start(A["out"][NTOK + a * 128:NTOK + (a + 1) * 128, :], T["zrow"][:]).then_inc(zero_out, 16)
            sp.wait_ge(b_in, 32)
            sp.wait_ge(zero_out, 16 * CAPT)

        @block.gpsimd
        def _(pool):
            pool.memset(T["ident"][:], 0.0).then_inc(cleared, 1)
            pool.wait_ge(cleared, 1)
            pool.affine_select(out=T["ident"][:], in_=T["ident"][:], compare_op=ALU.not_equal, fill=1.0, base=0,
                               pattern=[[-1, 128]], channel_multiplier=1).then_inc(ident_done, 1)
            pool.memset(T["mhalf"][:], -0.5).then_inc(ident_done, 1)
            pool.memset(T["eps"][:], EPS).then_inc(ident_done, 1)

        @block.vector
        def _(dve):
            nc.vector.memset(T["zrow"][:], 0.0).then_inc(zeroed, 1)
            nc.vector.memset(T["ones"][:], 1.0).then_inc(zeroed, 1)
            dve.wait_ge(mask_in, 16)
            nc.vector.tensor_reduce(m01[:, 0:1], mrow[:, 0:SK - NKEY], AX.X, ALU.max).then_inc(flag_step, 1)
            nc.vector.tensor_reduce(m01[:, 1:2], mrow[:, SK - NKEY:SK], AX.X, ALU.max).then_inc(flag_step, 1)
            dve.wait_ge(flag_step, 2)
            nc.vector.tensor_tensor(m01[:, 2:3], m01[:, 0:1], m01[:, 1:2], ALU.is_lt).then_inc(flag_step, 1)
            for c in range(14):
                dve.wait_ge(hi_done, c + 1)
                dst = T["w_lo"][:, c, :]
                nc.vector.tensor_tensor(dst, stage[:, c, :], f32(T["w_hi"][:, c, :]), ALU.subtract).then_inc(lo_done, 1)
            dve.wait_ge(flag_sum, 1)
            nc.vector.tensor_scalar(m01[0:1, 3:4], flag_ps[0:1, 0:1], float(B) - 0.5, None, ALU.is_gt).then_inc(flag_step, 1)
            dve.wait_ge(flag_step, 4)
            nc.vector.tensor_copy(T["flag"][:], m01[0:1, 3:4]).then_inc(flag_step, 1)
            dve.wait_ge(flag_step, 5)

        @block.scalar
        def _(act):
            for c in range(14):
                act.wait_ge(w_in, 16 * 4)
                nc.scalar.activation(T["w_hi"][:, c, :], stage[:, c, :], ACT.Copy).then_inc(hi_done, 1)

        @block.tensor
        def _(pe):
            pe.wait_ge(flag_step, 3)
            pe.wait_ge(zeroed, 2)
            nc.tensor.matmul(flag_ps[0:1, 0:1], m01[:, 2:3], T["ones"][0:B, 0:1], start=True, stop=True).then_inc(flag_sum, 1)


PRO_ORDER = [("fx", 0), ("fx", 1), ("fx", 2), ("fx", 3), ("fc", 0), ("fc", 1), ("fc", 2), ("v", 0), ("v", 1), ("q", 0), ("k", 0)]
ITER_ORDER = [("v", 2), ("v", 3), ("q", 1), ("k", 1), ("q", 2), ("k", 2), ("q", 3), ("k", 3),
              ("fx", 0), ("fx", 1), ("fx", 2), ("fx", 3), ("fc", 0), ("fc", 1), ("fc", 2), ("v", 0), ("v", 1),
              ("wo", 0), ("wo", 1), ("wo", 2), ("wo", 3), ("q", 0), ("k", 0),
              ("tt", 0), ("tt", 1), ("tt", 2), ("tt", 3), ("lg", 0)]
NPRO, NITER = len(PRO_ORDER), len(ITER_ORDER)
SPLIT = ("fx", "fc", "v", "q", "k")
HPRO = NPRO
HITER = sum(k in SPLIT for k, _ in ITER_ORDER)
LAST_ORDER = ITER_ORDER[:8] + ITER_ORDER[17:21] + ITER_ORDER[23:]
NU = 16
LT = 3


def steps(nxt):
    out = [("s", 0), ("s", 1), ("v", 2), ("v", 3), ("s", 2)]
    for u in range(3, NU):
        if u in (3, 6, 10):
            hp = {3: 1, 6: 2, 10: 3}[u]
            out += [("q", hp), ("k", hp)]
        out.append(("s", u))
        out.append(("t", u - LT))
        if u - LT - 1 >= 0:
            out.append(("o", u - LT - 1))
    if nxt:
        out += [("fx", 0), ("fx", 1), ("fx", 2), ("fx", 3)]
    out += [("t", 13), ("o", 12)]
    if nxt:
        out += [("fc", 0), ("fc", 1), ("fc", 2)]
    out += [("t", 14), ("o", 13), ("t", 15), ("o", 14), ("o", 15)]
    if nxt:
        out += [("v", 0), ("v", 1)]
    out += [("wo", 0), ("wo", 1), ("wo", 2), ("wo", 3)]
    if nxt:
        out += [("q", 0), ("k", 0)]
    out += [("tt", 0), ("tt", 1), ("tt", 2), ("tt", 3), ("lg", 0)]
    return out


def attention_short(nc, T, A):
    with ExitStack() as ctx:
        def sb(name, shape, dt=F32):
            return ctx.enter_context(nc.sbuf_tensor(name, shape, dt))

        def psum(name):
            return ctx.enter_context(nc.psum_tensor(name, [128, 512], F32))

        def sem(name):
            return ctx.enter_context(nc.semaphore(name))

        x_sb, c_sb = sb("x_sb", [R, TP, D]), sb("c_sb", [KC, TP, DC])
        m_sb, mb = sb("m_sb", [R, 2, NKEY], U8), sb("mask_bias", [R, 2, NKEY])
        xr = sb("x_res", [R, TP, D])
        xn2 = sb("xn2", [R, TP, D])
        xT = [sb(f"xT_{k}", [128, DCH, TP * R], F32R) for k in ("hi", "lo")]
        cT = [sb(f"cT_{k}", [128, CCH, TP * KC], F32R) for k in ("hi", "lo")]
        qz = [[sb(f"q{h}_{k}", [128, 2, TP * R], F32R) for k in ("hi", "lo")] for h in range(2)]
        kT = [sb(f"k_{k}", [128, 2, TP * KC], F32R) for k in ("hi", "lo")]
        v_sb = [sb(f"v_{k}", [KC, TP, HP, 192], F32R) for k in ("hi", "lo")]
        P = sb("probs", [R, 4, 2, NKEY])
        pT = [sb(f"pT_{k}", [KC, 2, 2 * S], F32R) for k in ("hi", "lo")]
        oT = [sb(f"oT_{k}", [128, HP, TP * R], F32R) for k in ("hi", "lo")]
        x2T = sb("x2T", [128, DCH, TP * R])
        lgT = sb("lgT", [E, TP * R])
        nmax, ssum, rsum = sb("nmax", [R, 4, 2]), sb("ssum", [R, 4, 2]), sb("rsum", [R, 4, 2])
        st1, mv1, rs1 = sb("st1", [R, TP, 6]), sb("mv1", [R, TP, 2]), sb("rs1", [R, TP])
        st2, mv2, rs2 = sb("st2", [R, TP, 6]), sb("mv2", [R, TP, 2]), sb("rs2", [R, TP])
        psS, psT = [psum("psS0"), psum("psS1")], [psum("psT0"), psum("psT1")]
        psO, psJ = [psum("psO0"), psum("psO1")], [psum("psJ0"), psum("psJ1")]

        x_in, c_in, m_in, xr_in = sem("x_in"), sem("c_in"), sem("m_in"), sem("xr_in")
        x2_out, xn2_out = sem("x2_out"), sem("xn2_out")
        proj_mm, proj_hi, proj_done = sem("proj_mm"), sem("proj_hi"), sem("proj_done")
        s_mm, masked, exped, recip, normed = sem("s_mm"), sem("masked"), sem("exped"), sem("recip"), sem("normed")
        t_mm, pt_hi, pt_lo = sem("t_mm"), sem("pt_hi"), sem("pt_lo")
        o_mm, o_hi, o_lo = sem("o_mm"), sem("o_hi"), sem("o_lo")
        st1_done, var1, eps1, rs1_done, xn_done = sem("st1_done"), sem("var1"), sem("eps1"), sem("rs1_done"), sem("xn_done")
        st2_done, var2, eps2, rs2_done, xn2_done = sem("st2_done"), sem("var2"), sem("eps2"), sem("rs2_done"), sem("xn2_done")
        biased, lg_copied, lg_t, mbias, zeros = sem("biased"), sem("lg_copied"), sem("lg_t"), sem("mbias"), sem("zeros")
        passed = sem("passed")

        rows = lambda ap, p, t=TP: ap.rearrange("(q t r) d -> q r t d", t=t, r=R)[bass.ds(p, 1)].rearrange("o r t d -> (o r) t d")

        def c_rows(p, b):
            v = A["ctx"].rearrange("(q b) (c r) d -> q b r c d", b=2, r=KC)[bass.ds(p, 1)]
            return v[:, b, :, SK // KC - 2:SK // KC, :].rearrange("o r c d -> (o r) c d")

        def m_row(p, b):
            v = A["mask"].rearrange("(q b) k -> q b k", b=2)[bass.ds(p, 1)]
            return v[:, b, SK - NKEY:SK].partition_broadcast(R)

        def order(nxt):
            return ITER_ORDER if nxt else LAST_ORDER

        def ring(p, nxt, kind, i):
            return PRO_ORDER.index((kind, i)) if p is None else order(nxt).index((kind, i)) + NPRO + NITER * p

        def bank(p, nxt, kind, i):
            return psJ[(PRO_ORDER.index((kind, i)) if p is None else order(nxt).index((kind, i)) + NPRO) % 2]

        def hi_count(p, nxt, kind, i):
            if p is None:
                return PRO_ORDER.index((kind, i)) + 1
            return [x for x in order(nxt) if x[0] in SPLIT].index((kind, i)) + 1 + HPRO + HITER * p

        def v_half(src, h):
            return src[0:KC, 0:D].rearrange("p (a h d) -> p a h d", h=2, d=DH)[:, :, h, :]

        block = ctx.enter_context(nc.Block())

        @block.sync
        def _(sp):
            def load_front(p):
                sp.dma_start(x_sb[:], rows(A["x"], p)).then_inc(x_in, 16)
                for b in range(2):
                    sp.dma_start(c_sb[:, 2 * b:2 * b + 2, :], c_rows(p, b)).then_inc(c_in, 16)

            def load_mask(p):
                for b in range(2):
                    sp.dma_start(m_sb[:, b, :], m_row(p, b)).then_inc(m_in, 16)

            def iteration(p, nxt):
                sp.dma_start(xr[:], rows(A["x"], p)).then_inc(xr_in, 16)
                if nxt:
                    sp.wait_ge(proj_mm, NPRO if isinstance(p, int) and p == 0 else ring(p - 1, True, "fc", 2) + 1)
                    load_front(p + 1)
                    sp.wait_ge(mbias, p + 1)
                    load_mask(p + 1)
                sp.wait_ge(proj_done, ring(p, nxt, "wo", TP - 1) + 1)
                sp.dma_start(rows(A["out"][0:NTOK, :], p), xr[:]).then_inc(x2_out, 16)
                sp.wait_ge(xn2_done, TP * p + TP)
                sp.dma_start(rows(A["xn2"], p), xn2[:]).then_inc(xn2_out, 16)
                sp.wait_ge(x2_out, 16 * p + 16)
                held(sp, passed, xn2_out, 16 * p + 16)

            load_front(0)
            load_mask(0)
            iteration(0, True)
            with sp.Fori(1, NPAIR - 1) as p:
                iteration(p, True)
            iteration(NPAIR - 1, False)

        @block.gpsimd
        def _(pool):
            def rstd(n, var_sem, mv, rs, e_sem, out_sem, cols):
                pool.wait_ge(var_sem, n)
                nc.gpsimd.tensor_tensor(rs, mv, T["eps"][0:R, 0:cols], ALU.add).then_inc(e_sem, 1)
                pool.wait_ge(e_sem, n)
                nc.gpsimd.tensor_tensor(rs, rs, T["mhalf"][0:R, 0:cols], ALU.pow).then_inc(out_sem, 1)

            def front_ln(n):
                rstd(n, var1, mv1[:, :, 1], rs1[:, :], eps1, rs1_done, TP)

            def iteration(p, nxt):
                pool.wait_ge(xr_in, 16 * p + 16)
                for t in range(TP):
                    nc.gpsimd.tensor_tensor(xr[:, t, :], xr[:, t, :], T["bias"][:], ALU.add).then_inc(biased, 1)
                for u in range(NU):
                    pool.wait_ge(recip, NU * p + u + 1)
                    nc.gpsimd.tensor_tensor(P[:, u % 4], P[:, u % 4], rsum[:, u % 4, :].unsqueeze(2).to_broadcast([R, 2, NKEY]),
                                            ALU.mult).then_inc(normed, 1)
                    if nxt and u == 9:
                        front_ln(p + 2)
                for t in range(TP):
                    rstd(TP * p + t + 1, var2, mv2[:, t, 1:2], rs2[:, t:t + 1], eps2, rs2_done, 1)

            front_ln(1)
            iteration(0, True)
            with pool.Fori(1, NPAIR - 1) as p:
                iteration(p, True)
            iteration(NPAIR - 1, False)

        @block.scalar
        def _(act):
            def split_hi(p, nxt, kind, i):
                act.wait_ge(proj_mm, ring(p, nxt, kind, i) + 1)
                src = bank(p, nxt, kind, i)
                if kind == "fx":
                    nc.scalar.activation(xT[0][:, i, :], src[:, 0:TP * R], ACT.Copy).then_inc(proj_hi, 1)
                elif kind == "fc":
                    nc.scalar.activation(cT[0][:, i, :], src[:, 0:TP * KC], ACT.Copy).then_inc(proj_hi, 1)
                elif kind == "v":
                    nc.scalar.activation(v_sb[0][:, i, :, 0:64], v_half(src, 0), ACT.Copy)
                    nc.scalar.activation(v_sb[0][:, i, :, 128:192], v_half(src, 1), ACT.Copy).then_inc(proj_hi, 1)
                elif kind == "q":
                    nc.scalar.activation(qz[0][0][0:64, i % 2, :], src[0:64, 0:TP * R], ACT.Copy)
                    nc.scalar.activation(qz[1][0][64:128, i % 2, :], src[64:128, 0:TP * R], ACT.Copy).then_inc(proj_hi, 1)
                else:
                    nc.scalar.activation(kT[0][:, i % 2, :], src[:, 0:TP * KC], ACT.Copy).then_inc(proj_hi, 1)

            def iteration(p, nxt):
                for kind, i in steps(nxt):
                    if kind in SPLIT:
                        split_hi(p, nxt, kind, i)
                    elif kind == "s":
                        act.wait_ge(masked, NU * p + i + 1)
                        for it in range(2):
                            e = nc.scalar.activation(P[:, i % 4, it, :], P[:, i % 4, it, :], ACT.Exp,
                                                     bias=nmax[:, i % 4, it:it + 1], scale=-1.0,
                                                     accum_out=ssum[:, i % 4, it:it + 1])
                        e.then_inc(exped, 1)
                    elif kind == "t":
                        act.wait_ge(t_mm, NU * p + i + 1)
                        nc.scalar.activation(pT[0][:, i % 2, :], psT[i % 2][0:KC, 0:2 * S], ACT.Copy).then_inc(pt_hi, 1)
                    elif kind == "o" and i % 2:
                        j, hp, b = i // 2, i // 4, (i // 2) % 2
                        act.wait_ge(o_mm, NU // 2 * p + j + 1)
                        nc.scalar.activation(oT[0][:, hp, b * S:(b + 1) * S], psO[j % 2][:, 0:S], ACT.Copy).then_inc(o_hi, 1)

            for kind, i in PRO_ORDER:
                if kind == "v" and i == 0:
                    act.wait_ge(zeros, 4)
                split_hi(None, True, kind, i)
            iteration(0, True)
            with act.Fori(1, NPAIR - 1) as p:
                iteration(p, True)
            iteration(NPAIR - 1, False)

        @block.vector
        def _(dve):
            def split_lo(p, nxt, kind, i):
                dve.wait_ge(proj_hi, hi_count(p, nxt, kind, i))
                src = bank(p, nxt, kind, i)
                if kind == "fx":
                    a, h, o = src[:, 0:TP * R], xT[0][:, i, :], xT[1][:, i, :]
                elif kind == "fc":
                    a, h, o = src[:, 0:TP * KC], cT[0][:, i, :], cT[1][:, i, :]
                elif kind == "v":
                    nc.vector.tensor_tensor(v_sb[1][:, i, :, 0:64], v_half(src, 0), f32(v_sb[0][:, i, :, 0:64]), ALU.subtract)
                    a, h, o = v_half(src, 1), v_sb[0][:, i, :, 128:192], v_sb[1][:, i, :, 128:192]
                elif kind == "q":
                    nc.vector.tensor_tensor(qz[0][1][0:64, i % 2, :], src[0:64, 0:TP * R], f32(qz[0][0][0:64, i % 2, :]), ALU.subtract)
                    a, h, o = src[64:128, 0:TP * R], qz[1][0][64:128, i % 2, :], qz[1][1][64:128, i % 2, :]
                else:
                    a, h, o = src[:, 0:TP * KC], kT[0][:, i % 2, :], kT[1][:, i % 2, :]
                nc.vector.tensor_tensor(o, a, f32(h), ALU.subtract).then_inc(proj_done, 1)

            def front_stats(n):
                dve.wait_ge(x_in, 16 * n)
                for t in range(TP):
                    s = nc.vector.bn_stats(st1[:, t, :], x_sb[:, t, :])
                s.then_inc(st1_done, 1)
                held(dve, passed, st1_done, n)
                for t in range(TP):
                    s = nc.vector.bn_aggr(mv1[:, t, :], st1[:, t, :])
                s.then_inc(var1, 1)

            def front_apply(n):
                dve.wait_ge(rs1_done, n)
                for t in range(TP):
                    s = nc.vector.tensor_scalar(x_sb[:, t, :], x_sb[:, t, :], mv1[:, t, 0:1], rs1[:, t:t + 1],
                                                ALU.subtract, ALU.mult)
                s.then_inc(xn_done, 1)

            def mask_bias(n):
                dve.wait_ge(m_in, 32 * n)
                nc.vector.tensor_scalar(mb[:], m_sb[:], 1.0, BIG, ALU.subtract, ALU.mult).then_inc(mbias, 1)
                dve.wait_ge(mbias, n)

            def reciprocal(p, u):
                dve.wait_ge(exped, NU * p + u + 1)
                nc.vector.reciprocal(rsum[:, u % 4, :], ssum[:, u % 4, :]).then_inc(recip, 1)

            def tail_stats(p, nxt, t):
                dve.wait_ge(proj_mm, ring(p, nxt, "wo", t) + 1)
                if t == 0:
                    dve.wait_ge(biased, TP * p + TP)
                nc.vector.tensor_tensor(xr[:, t, :], bank(p, nxt, "wo", t)[0:R, :], xr[:, t, :], ALU.add).then_inc(proj_done, 1)
                dve.wait_ge(proj_done, ring(p, nxt, "wo", t) + 1)
                nc.vector.bn_stats(st2[:, t, :], xr[:, t, :]).then_inc(st2_done, 1)
                held(dve, passed, st2_done, TP * p + t + 1)
                nc.vector.bn_aggr(mv2[:, t, :], st2[:, t, :]).then_inc(var2, 1)

            def tail_apply(p, t):
                dve.wait_ge(rs2_done, TP * p + t + 1)
                nc.vector.tensor_scalar(xn2[:, t, :], xr[:, t, :], mv2[:, t, 0:1], rs2[:, t:t + 1],
                                        ALU.subtract, ALU.mult).then_inc(xn2_done, 1)

            def iteration(p, nxt):
                for kind, i in steps(nxt):
                    if kind in SPLIT:
                        split_lo(p, nxt, kind, i)
                    elif kind == "s":
                        held(dve, passed, s_mm, NU * p + i + 1)
                        b = (i // 2) % 2
                        for it in range(2):
                            s = nc.vector.tensor_tensor_reduce(
                                out=P[:, i % 4, it, :], in0=psS[i % 2][0:R, it * NKEY:(it + 1) * NKEY], in1=mb[:, b, :],
                                scale=SCALE, scalar=BIG, op0=ALU.add, op1=ALU.min, accum_out=nmax[:, i % 4, it:it + 1])
                        s.then_inc(masked, 1)
                        if i >= 1:
                            reciprocal(p, i - 1)
                        if i == NU - 1:
                            reciprocal(p, i)
                        if nxt and i == 8:
                            front_stats(p + 2)
                        if nxt and i == 12:
                            front_apply(p + 2)
                    elif kind == "t":
                        dve.wait_ge(pt_hi, NU * p + i + 1)
                        nc.vector.tensor_tensor(pT[1][:, i % 2, :], psT[i % 2][0:KC, 0:2 * S], f32(pT[0][:, i % 2, :]),
                                                ALU.subtract).then_inc(pt_lo, 1)
                    elif kind == "o" and i % 2:
                        j, hp, b = i // 2, i // 4, (i // 2) % 2
                        dve.wait_ge(o_hi, NU // 2 * p + j + 1)
                        nc.vector.tensor_tensor(oT[1][:, hp, b * S:(b + 1) * S], psO[j % 2][:, 0:S],
                                                f32(oT[0][:, hp, b * S:(b + 1) * S]), ALU.subtract).then_inc(o_lo, 1)
                    elif kind == "wo":
                        tail_stats(p, nxt, i)
                        if i:
                            tail_apply(p, i - 1)
                        if i == TP - 1:
                            tail_apply(p, i)
                            if nxt:
                                mask_bias(p + 2)
                    elif kind == "tt":
                        dve.wait_ge(proj_mm, ring(p, nxt, "tt", i) + 1)
                        src = bank(p, nxt, "tt", i)[:, 0:DCH * R].rearrange("p (c r) -> p c r", c=DCH)
                        nc.vector.tensor_copy(x2T[:, :, i * R:(i + 1) * R], src).then_inc(proj_done, 1)
                    elif kind == "lg":
                        dve.wait_ge(proj_mm, ring(p, nxt, "lg", 0) + 1)
                        src = bank(p, nxt, "lg", 0)
                        nc.vector.tensor_copy(lgT[:], src[0:E, 0:TP * R]).then_inc(lg_copied, 1)
                        dve.wait_ge(lg_t, p + 1)
                        nc.vector.tensor_copy(
                            T["logits"][:, :, bass.ds(p * TP, TP)].rearrange("p e t -> p t e"),
                            src[0:R, TP * R:TP * R + TP * E].rearrange("p (t e) -> p t e", e=E)).then_inc(proj_done, 1)

            for h, rows_ in ((0, slice(64, 128)), (1, slice(0, 64))):
                for k in range(2):
                    s = nc.vector.memset(f32(qz[h][k][rows_, :, :]), 0.0).then_inc(zeros, 1)
            for k in range(2):
                nc.vector.memset(f32(v_sb[k][:, :, :, 64:128]), 0.0).then_inc(zeros, 1)
            mask_bias(1)
            front_stats(1)
            front_apply(1)
            for kind, i in PRO_ORDER:
                split_lo(None, True, kind, i)
            iteration(0, True)
            with dve.Fori(1, NPAIR - 1) as p:
                iteration(p, True)
            iteration(NPAIR - 1, False)

        @block.tensor
        def _(pe):
            ident = T["ident"]

            def product(out, stationary, moving, n, first=True, last=True):
                for c in range(n):
                    for j, (a, b) in enumerate(((0, 0), (0, 1), (1, 0))):
                        mm = nc.tensor.matmul(out, stationary(a, c), moving(b, c), start=first and c == 0 and j == 0,
                                              stop=last and c == n - 1 and j == 2, skip_group_check=True)
                return mm

            def w(name):
                at, n = {"wq": (0, DCH), "wk": (4, CCH), "wv": (7, CCH), "wo": (10, DCH)}[name]
                return [T["w_hi"][:, at:at + n, :], T["w_lo"][:, at:at + n, :]]

            wq, wk, wv, wo = w("wq"), w("wk"), w("wv"), w("wo")

            def proj(p, nxt, kind, i, n):
                at = ring(p, nxt, kind, i)
                out = bank(p, nxt, kind, i)
                if p is not None or at >= 2:
                    pe.wait_ge(proj_done, at - 1)
                if kind == "fx":
                    pe.wait_ge(xn_done, n)
                    for t in range(TP):
                        mm = nc.tensor.transpose(out[:, t * R:(t + 1) * R], x_sb[:, t, i * 128:(i + 1) * 128], ident[0:R, 0:R])
                elif kind == "fc":
                    pe.wait_ge(c_in, 32 * n)
                    for j in range(TP):
                        mm = nc.tensor.transpose(out[:, j * KC:(j + 1) * KC], c_sb[:, j, i * 128:(i + 1) * 128], ident[0:KC, 0:KC])
                elif kind == "v":
                    if i == 0:
                        pe.wait_ge(proj_done, ring(p, nxt, "fc", CCH - 1) + 1)
                    mm = product(out[0:KC, :], lambda k, c: cT[k][:, c, i * KC:(i + 1) * KC], lambda k, c: wv[k][:, c, :], CCH)
                elif kind == "q":
                    mm = product(out[:, 0:TP * R], lambda k, c: wq[k][:, c, i * 128:(i + 1) * 128], lambda k, c: xT[k][:, c, :], DCH)
                elif kind == "k":
                    mm = product(out[:, 0:TP * KC], lambda k, c: wk[k][:, c, i * 128:(i + 1) * 128], lambda k, c: cT[k][:, c, :], CCH)
                elif kind == "wo":
                    if i == 0:
                        pe.wait_ge(o_lo, NU // 2 * p + NU // 2)
                    mm = product(out[0:R, :], lambda k, c: oT[k][:, c, i * R:(i + 1) * R], lambda k, c: wo[k][:, c, :], HP)
                elif kind == "tt":
                    pe.wait_ge(xn2_done, TP * p + i + 1)
                    for c in range(DCH):
                        mm = nc.tensor.transpose(out[:, c * R:(c + 1) * R], xn2[:, i, c * 128:(c + 1) * 128], ident[0:R, 0:R])
                else:
                    pe.wait_ge(proj_done, ring(p, nxt, "tt", TP - 1) + 1)
                    for c in range(DCH):
                        mm = nc.tensor.matmul(out[0:E, 0:TP * R], T["wr"][:, c, :], x2T[:, c, :], start=c == 0, stop=c == DCH - 1)
                mm.then_inc(proj_mm, 1)
                if kind == "lg":
                    held(pe, passed, lg_copied, p + 1)
                    for t in range(TP):
                        mm = nc.tensor.transpose(out[0:R, TP * R + t * E:TP * R + (t + 1) * E], lgT[:, t * R:(t + 1) * R], ident[0:E, 0:E])
                    mm.then_inc(lg_t, 1)

            def iteration(p, nxt):
                for kind, i in steps(nxt):
                    hp, b, h = i // 4, (i // 2) % 2, i % 2
                    if kind == "s":
                        if i == 0:
                            first = isinstance(p, int) and p == 0
                            pe.wait_ge(proj_done, (ring(None, True, "k", 0) if first else ring(p - 1, True, "k", 0)) + 1)
                        elif i % 4 == 0:
                            pe.wait_ge(proj_done, ring(p, nxt, "k", hp) + 1)
                        if i >= 2:
                            pe.wait_ge(masked, NU * p + i - 1)
                        for it in range(2):
                            at = b * S + it * R
                            mm = product(psS[i % 2][0:R, it * NKEY:(it + 1) * NKEY],
                                         lambda k, c: qz[h][k][:, hp % 2, at:at + R],
                                         lambda k, c: kT[k][:, hp % 2, b * NKEY:(b + 1) * NKEY], 1)
                        mm.then_inc(s_mm, 1)
                    elif kind == "t":
                        pe.wait_ge(normed, NU * p + i + 1)
                        if i >= 2:
                            pe.wait_ge(pt_lo, NU * p + i - 1)
                        for c in range(2):
                            for it in range(2):
                                mm = nc.tensor.transpose(psT[i % 2][0:KC, c * S + it * R:c * S + (it + 1) * R],
                                                         P[:, i % 4, it, c * KC:(c + 1) * KC], ident[0:R, 0:R])
                        mm.then_inc(t_mm, 1)
                    elif kind == "o":
                        pe.wait_ge(pt_lo, NU * p + i + 1)
                        if i == 2:
                            pe.wait_ge(proj_done, ring(p, nxt, "v", 3) + 1)
                        if i % 2 == 0 and i >= 4:
                            pe.wait_ge(o_lo, NU // 2 * p + i // 2 - 1)
                        mm = product(psO[(i // 2) % 2][:, 0:S], lambda k, c: v_sb[k][:, 2 * b + c, hp, h * DH:h * DH + 128],
                                     lambda k, c: pT[k][:, i % 2, c * S:(c + 1) * S], 2, first=h == 0, last=h == 1)
                        if h:
                            mm.then_inc(o_mm, 1)
                    else:
                        proj(p, nxt, kind, i, p + 2)

            pe.wait_ge(zeros, 6)
            for kind, i in PRO_ORDER:
                proj(None, True, kind, i, 1)
            iteration(0, True)
            with pe.Fori(1, NPAIR - 1) as p:
                iteration(p, True)
            iteration(NPAIR - 1, False)


GSTEPS = 5 + 2 * H + 2


def general_order():
    out = [("xT", c, 0) for c in range(DCH)] + [("cT", c, 0) for c in range(CCH)] + [("v", j, 0) for j in range(SK // KC)]
    for h in range(H):
        out += [("q", h, 0), ("k", h, 0)]
        for it in range(2):
            out += [("s", h, it), ("pT", h, it), ("o", h, it)]
    for it in range(2):
        out += [("oT", 0, it), ("wo", 0, it), ("x2T", 0, it), ("lg", 0, it)]
    return out


def attention_general(nc, T, A):
    with ExitStack() as ctx:
        def sb(name, shape, dt=F32):
            return ctx.enter_context(nc.sbuf_tensor(f"g_{name}", shape, dt))

        def sem(name):
            return ctx.enter_context(nc.semaphore(f"g_{name}"))

        NK, HALF = SK // KC, SK // 2
        ORDER = general_order()
        w = sb("w", [128, 14, D])
        wq, wk, wv, wo = w[:, 0:4, :], w[:, 4:7, :], w[:, 7:10, :], w[:, 10:14, :]
        x_sb, xr, xn2, c_sb = sb("x", [R, 2, D]), sb("xr", [R, 2, D]), sb("xn2", [R, 2, D]), sb("c", [KC, NK, DC])
        m_sb, mb, P = sb("m", [R, SK], U8), sb("mask_bias", [R, SK]), sb("probs", [R, SK])
        xT, cT = sb("xT", [128, DCH, 2 * R]), sb("cT", [128, CCH, SK])
        qT, kT, v_sb = sb("qT", [DH, 2 * R]), sb("kT", [DH, SK]), sb("v", [KC, NK, D])
        pT, o_sb, oT, x2T = sb("pT", [KC, NK, R]), sb("o", [R, 2, D]), sb("oT", [128, DCH, R]), sb("x2T", [128, DCH, R])
        nmin, ssum = sb("nmin", [R, 3]), sb("ssum", [R, 2])
        st, mv, rs = sb("st", [R, 2, 6]), sb("mv", [R, 2, 2]), sb("rs", [R, 2])
        ps = [ctx.enter_context(nc.psum_tensor(f"g_ps{i}", [128, 512], F32)) for i in range(2)]
        w_in, x_in, c_in, m_in, xr_in, out_done, xn2_out = (sem("w_in"), sem("x_in"), sem("c_in"), sem("m_in"), sem("xr_in"),
                                                            sem("out_done"), sem("xn2_out"))
        made, taken, step, masked, exped, normed = sem("made"), sem("taken"), sem("step"), sem("masked"), sem("exped"), sem("normed")
        passed = sem("passed")
        var, eps, rs_done, xn_done, x2_done, xn2_done = (sem("var"), sem("eps"), sem("rs_done"), sem("xn_done"), sem("x2_done"),
                                                         sem("xn2_done"))
        N = len(ORDER)
        TAKEN = N - 2
        block = ctx.enter_context(nc.Block())

        @block.sync
        def _(sp):
            at = 0
            for name, n in (("wq", DCH), ("wk", CCH), ("wv", CCH), ("wo", DCH)):
                sp.dma_start(w[:, at:at + n, :], A[name].rearrange("(c p) n -> p c n", p=128)).then_inc(w_in, 16)
                at += n
            with sp.Fori(0, B) as b:
                rows = lambda ap: ap.rearrange("(q t r) d -> q r t d", t=2, r=R)[bass.ds(b, 1)].rearrange("o r t d -> (o r) t d")
                sp.wait_ge(taken, 1 + TAKEN * b)
                sp.dma_start(x_sb[:], rows(A["x"])).then_inc(x_in, 16)
                sp.dma_start(xr[:], rows(A["x"])).then_inc(xr_in, 16)
                sp.dma_start(c_sb[:], A["ctx"].rearrange("q (c r) d -> q r c d", r=KC)[bass.ds(b, 1)]
                             .rearrange("o r c d -> (o r) c d")).then_inc(c_in, 16)
                sp.dma_start(m_sb[:], A["mask"][bass.ds(b, 1), :].partition_broadcast(R)).then_inc(m_in, 16)
                sp.wait_ge(x2_done, 2 * b + 2)
                sp.dma_start(rows(A["out"][0:NTOK, :]), xr[:]).then_inc(out_done, 16)
                sp.wait_ge(xn2_done, 2 * b + 2)
                sp.dma_start(rows(A["xn2"]), xn2[:]).then_inc(xn2_out, 16)
                sp.wait_ge(out_done, 16 * b + 16)
                held(sp, passed, xn2_out, 16 * b + 16)

        @block.gpsimd
        def _(pool):
            def rstd(n, cols, v, r):
                pool.wait_ge(var, n)
                nc.gpsimd.tensor_tensor(r, v, T["eps"][0:R, 0:cols], ALU.add).then_inc(eps, 1)
                pool.wait_ge(eps, n)
                nc.gpsimd.tensor_tensor(r, r, T["mhalf"][0:R, 0:cols], ALU.pow).then_inc(rs_done, 1)

            with pool.Fori(0, B) as b:
                rstd(3 * b + 1, 2, mv[:, :, 1], rs[:, :])
                for it in range(2):
                    rstd(3 * b + it + 2, 1, mv[:, it, 1:2], rs[:, it:it + 1])

        @block.scalar
        def _(act):
            with act.Fori(0, B) as b:
                for i in range(2 * H):
                    act.wait_ge(masked, 2 * H * b + i + 1)
                    nc.scalar.activation(P[:], P[:], ACT.Exp, bias=nmin[:, 2:3], scale=-1.0, accum_out=ssum[:, 0:1]).then_inc(exped, 1)

        @block.vector
        def _(dve):
            dve.sem_inc(taken, 1)
            with dve.Fori(0, B) as b:
                done = [0]

                def then(ins):
                    done[0] += 1
                    ins.then_inc(step, 1)
                    held(dve, passed, step, GSTEPS * b + done[0])

                dve.wait_ge(m_in, 16 * b + 16)
                then(nc.vector.tensor_scalar(mb[:], m_sb[:], 1.0, BIG, ALU.subtract, ALU.mult))
                dve.wait_ge(x_in, 16 * b + 16)
                for it in range(2):
                    then(nc.vector.bn_stats(st[:, it, :], x_sb[:, it, :]))
                nc.vector.bn_aggr(mv[:, 0, :], st[:, 0, :])
                nc.vector.bn_aggr(mv[:, 1, :], st[:, 1, :]).then_inc(var, 1)
                dve.wait_ge(rs_done, 3 * b + 1)
                for it in range(2):
                    nc.vector.tensor_scalar(x_sb[:, it, :], x_sb[:, it, :], mv[:, it, 0:1], rs[:, it:it + 1],
                                            ALU.subtract, ALU.mult).then_inc(xn_done, 1)
                dve.wait_ge(xr_in, 16 * b + 16)
                for it in range(2):
                    then(nc.vector.tensor_tensor(xr[:, it, :], xr[:, it, :], T["bias"][:], ALU.add))
                for n, (kind, i, it) in enumerate(ORDER):
                    if kind == "s":
                        held(dve, passed, made, N * b + n + 1)
                    else:
                        dve.wait_ge(made, N * b + n + 1)
                    if kind == "xT":
                        last = nc.vector.tensor_copy(xT[:, i, :], ps[0][:, 0:2 * R])
                    elif kind == "cT":
                        nc.vector.tensor_copy(cT[:, i, 0:HALF], ps[0][:, 0:HALF])
                        last = nc.vector.tensor_copy(cT[:, i, HALF:SK], ps[1][:, 0:HALF])
                    elif kind == "v":
                        last = nc.vector.tensor_copy(v_sb[:, i, :], ps[0][0:KC, :])
                    elif kind == "q":
                        last = nc.vector.tensor_copy(qT[:], ps[0][0:DH, 0:2 * R])
                    elif kind == "k":
                        nc.vector.tensor_copy(kT[:, 0:HALF], ps[0][0:DH, 0:HALF])
                        last = nc.vector.tensor_copy(kT[:, HALF:SK], ps[1][0:DH, 0:HALF])
                    elif kind == "s":
                        for k in range(2):
                            s = nc.vector.tensor_tensor_reduce(
                                out=P[:, k * HALF:(k + 1) * HALF], in0=ps[k][0:R, 0:HALF], in1=mb[:, k * HALF:(k + 1) * HALF],
                                scale=SCALE, scalar=BIG, op0=ALU.add, op1=ALU.min, accum_out=nmin[:, k:k + 1])
                        then(s)
                        nc.vector.tensor_tensor(nmin[:, 2:3], nmin[:, 0:1], nmin[:, 1:2], ALU.min).then_inc(masked, 1)
                        dve.wait_ge(exped, 2 * H * b + 2 * i + it + 1)
                        nc.vector.reciprocal(ssum[:, 1:2], ssum[:, 0:1]).then_inc(normed, 1)
                        dve.wait_ge(normed, 2 * H * b + 2 * i + it + 1)
                        last = nc.vector.tensor_scalar(P[:], P[:], ssum[:, 1:2], None, ALU.mult)
                    elif kind == "pT":
                        for k in range(2):
                            last = nc.vector.tensor_copy(pT[:, k * NK // 2:(k + 1) * NK // 2, :],
                                                         ps[k][0:KC, 0:NK // 2 * R].rearrange("p (c r) -> p c r", r=R))
                    elif kind == "o":
                        last = nc.vector.tensor_copy(o_sb[:, it, i * DH:(i + 1) * DH], ps[0][0:R, 0:DH])
                    elif kind == "oT":
                        last = nc.vector.tensor_copy(oT[:], ps[0][:, 0:DCH * R].rearrange("p (c r) -> p c r", r=R))
                    elif kind == "wo":
                        nc.vector.tensor_tensor(xr[:, it, :], ps[0][0:R, :], xr[:, it, :], ALU.add).then_inc(x2_done, 1)
                        dve.wait_ge(x2_done, 2 * b + it + 1)
                        then(nc.vector.bn_stats(st[:, it, :], xr[:, it, :]))
                        nc.vector.bn_aggr(mv[:, it, :], st[:, it, :]).then_inc(var, 1)
                        dve.wait_ge(rs_done, 3 * b + it + 2)
                        nc.vector.tensor_scalar(xn2[:, it, :], xr[:, it, :], mv[:, it, 0:1], rs[:, it:it + 1],
                                                ALU.subtract, ALU.mult).then_inc(xn2_done, 1)
                    elif kind == "x2T":
                        last = nc.vector.tensor_copy(x2T[:], ps[0][:, 0:DCH * R].rearrange("p (c r) -> p c r", r=R))
                    else:
                        last = nc.vector.tensor_copy(T["logits"][:, :, bass.ds(2 * b + it, 1)].rearrange("p e o -> p (e o)"),
                                                     ps[0][0:R, 0:E])
                    if kind != "wo":
                        last.then_inc(taken, 1)
                assert done[0] == GSTEPS

        @block.tensor
        def _(pe):
            ident = T["ident"]

            def product(out, stationary, moving, n):
                for c in range(n):
                    mm = nc.tensor.matmul(out, stationary(c), moving(c), start=c == 0, stop=c == n - 1)
                return mm

            pe.wait_ge(w_in, 64)
            with pe.Fori(0, B) as b:
                for n, (kind, i, it) in enumerate(ORDER):
                    pe.wait_ge(taken, 1 + TAKEN * b + sum(k != "wo" for k, _, _ in ORDER[:n]))
                    if kind == "x2T":
                        pe.wait_ge(xn2_done, 2 * b + it + 1)
                    mine = slice(it * R, (it + 1) * R)
                    if kind == "xT":
                        pe.wait_ge(xn_done, 2 * b + 2)
                        for t in range(2):
                            mm = nc.tensor.transpose(ps[0][:, t * R:(t + 1) * R], x_sb[:, t, i * 128:(i + 1) * 128], ident[0:R, 0:R])
                    elif kind == "cT":
                        pe.wait_ge(c_in, 16 * b + 16)
                        for j in range(NK):
                            at = j % (NK // 2) * KC
                            mm = nc.tensor.transpose(ps[j // (NK // 2)][:, at:at + KC], c_sb[:, j, i * 128:(i + 1) * 128],
                                                     ident[0:KC, 0:KC])
                    elif kind == "v":
                        mm = product(ps[0][0:KC, :], lambda c: cT[:, c, i * KC:(i + 1) * KC], lambda c: wv[:, c, :], CCH)
                    elif kind == "q":
                        mm = product(ps[0][0:DH, 0:2 * R], lambda c: wq[:, c, i * DH:(i + 1) * DH], lambda c: xT[:, c, :], DCH)
                    elif kind == "k":
                        for k in range(2):
                            mm = product(ps[k][0:DH, 0:HALF], lambda c: wk[:, c, i * DH:(i + 1) * DH],
                                         lambda c: cT[:, c, k * HALF:(k + 1) * HALF], CCH)
                    elif kind == "s":
                        for k in range(2):
                            mm = nc.tensor.matmul(ps[k][0:R, 0:HALF], qT[:, mine], kT[:, k * HALF:(k + 1) * HALF], start=True, stop=True)
                    elif kind == "pT":
                        for j in range(NK):
                            at = j % (NK // 2) * R
                            mm = nc.tensor.transpose(ps[j // (NK // 2)][0:KC, at:at + R], P[:, j * KC:(j + 1) * KC], ident[0:R, 0:R])
                    elif kind == "o":
                        mm = product(ps[0][0:R, 0:DH], lambda c: pT[:, c, :], lambda c: v_sb[:, c, i * DH:(i + 1) * DH], NK)
                    elif kind in ("oT", "x2T"):
                        src = o_sb if kind == "oT" else xn2
                        for c in range(DCH):
                            mm = nc.tensor.transpose(ps[0][:, c * R:(c + 1) * R], src[:, it, c * 128:(c + 1) * 128], ident[0:R, 0:R])
                    elif kind == "wo":
                        mm = product(ps[0][0:R, :], lambda c: oT[:, c, :], lambda c: wo[:, c, :], DCH)
                    else:
                        mm = product(ps[0][0:R, 0:E], lambda c: x2T[:, c, :], lambda c: T["wr"][:, c, :], DCH)
                    mm.then_inc(made, 1)


def over_experts(ap):
    return ap.rearrange("p e t -> p t e")


def each_expert(ap):
    return ap.unsqueeze(1).to_broadcast([R, E, NT])


def each_token(ap):
    return ap.unsqueeze(2).to_broadcast([R, E, NT])


def flat(ap):
    return ap.rearrange("p e t -> p (e t)")


def router(nc, T):
    with ExitStack() as ctx:
        def sb(name, shape, dt=F32):
            return ctx.enter_context(nc.sbuf_tensor(name, shape, dt))

        def sem(name):
            return ctx.enter_context(nc.semaphore(name))

        z, probs, rest = sb("z", [R, E, NT]), sb("router_probs", [R, E, NT]), sb("rest", [R, E, NT])
        eq, rank, sel = sb("eq", [R, E, NT]), sb("rank", [R, E, NT]), sb("sel", [R, 2, E, NT])
        rank_i, id_i = sb("rank_i", [R, E, NT], I32), sb("id_i", [R, NT], I32)
        iota_i, iota_t, dump_i = sb("iota_i", [R, 128], I32), sb("iota_t_i", [R, CAPT], I32), sb("dump_i", [128, CAPT], I32)
        red, cnt, over = sb("red", [R, 4, NT]), sb("cnt", [R, E]), sb("over", [1, 2])
        ps = ctx.enter_context(nc.psum_tensor("count_ps", [128, 512], F32))
        iotas, consts, step, shifted, exped, counted = (sem("iotas"), sem("consts"), sem("step"), sem("shifted"),
                                                        sem("exped"), sem("counted"))
        block = ctx.enter_context(nc.Block())

        @block.gpsimd
        def _(pool):
            nc.gpsimd.iota(rank_i[:], pattern=[[-1, E], [0, NT]], base=E, channel_multiplier=0).then_inc(iotas, 1)
            nc.gpsimd.iota(id_i[:], pattern=[[R, NT]], base=0, channel_multiplier=1).then_inc(iotas, 1)
            nc.gpsimd.iota(iota_i[:], pattern=[[1, 128]], base=0, channel_multiplier=0).then_inc(iotas, 1)
            nc.gpsimd.iota(iota_t[:], pattern=[[1, CAPT]], base=0, channel_multiplier=0).then_inc(iotas, 1)
            nc.gpsimd.iota(dump_i[:], pattern=[[128, CAPT]], base=NTOK, channel_multiplier=1).then_inc(iotas, 1)
            nc.gpsimd.memset(T["ones_m"][:], 1.0).then_inc(consts, 1)
            nc.gpsimd.memset(T["after"][:], 1.0).then_inc(consts, 1)
            nc.gpsimd.memset(T["not_first"][:], 1.0).then_inc(consts, 1)
            pool.wait_ge(consts, 3)
            nc.gpsimd.affine_select(out=T["after"][:], in_=T["after"][:], compare_op=ALU.is_gt, fill=0.0, base=0,
                                    pattern=[[1, R]], channel_multiplier=-1).then_inc(consts, 1)
            nc.gpsimd.memset(T["not_first"][:, :, 0:1], 0.0).then_inc(consts, 1)

        @block.vector
        def _(dve):
            done = [0]

            def then(ins):
                done[0] += 1
                ins.then_inc(step, 1)
                dve.wait_ge(step, done[0])

            logits = T["logits"]
            dve.wait_ge(iotas, 5)
            nc.vector.tensor_copy(rank[:], rank_i[:])
            nc.vector.tensor_copy(T["iota"][:], iota_i[:])
            nc.vector.tensor_copy(T["iota_t"][:], iota_t[:])
            nc.vector.tensor_copy(T["dump"][:], dump_i[:])
            nc.vector.tensor_copy(T["vals"][:, :, :, 0], each_expert(id_i[:]))
            nc.vector.memset(T["vals"][:, :, :, 3], 1.0)
            then(nc.vector.tensor_reduce(red[:, 0, :], over_experts(logits[:]), AX.X, ALU.max))
            nc.vector.tensor_tensor(z[:], logits[:], each_expert(red[:, 0, :]), ALU.subtract).then_inc(shifted, 1)
            dve.wait_ge(exped, 1)
            then(nc.vector.tensor_reduce(red[:, 1, :], over_experts(z[:]), AX.X, ALU.add))
            then(nc.vector.reciprocal(red[:, 2, :], red[:, 1, :]))
            then(nc.vector.tensor_tensor(probs[:], z[:], each_expert(red[:, 2, :]), ALU.mult))
            src = probs
            for k in range(2):
                then(nc.vector.tensor_reduce(red[:, 0, :], over_experts(src[:]), AX.X, ALU.max))
                then(nc.vector.tensor_tensor(eq[:], src[:], each_expert(red[:, 0, :]), ALU.is_equal))
                then(nc.vector.tensor_tensor(eq[:], eq[:], rank[:], ALU.mult))
                then(nc.vector.tensor_reduce(red[:, 3, :], over_experts(eq[:]), AX.X, ALU.max))
                then(nc.vector.tensor_tensor(sel[:, k], rank[:], each_expert(red[:, 3, :]), ALU.is_equal))
                if k == 0:
                    then(nc.vector.scalar_tensor_tensor(out=flat(rest[:]), in0=flat(sel[:, 0]), scalar=-2.0, in1=flat(probs[:]),
                                                        op0=ALU.mult, op1=ALU.add))
                    src = rest
            then(nc.vector.tensor_tensor(T["has"][:], sel[:, 0], sel[:, 1], ALU.add))
            then(nc.vector.tensor_tensor(T["gate"][:], probs[:], T["has"][:], ALU.mult))
            nc.vector.tensor_copy(T["gate_hi"][:], T["gate"][:])
            nc.vector.tensor_copy(T["keep"][:], T["has"][:])
            then(nc.vector.tensor_reduce(cnt[:], T["has"][:], AX.X, ALU.add))
            nc.vector.tensor_copy(T["vals"][:, :, :, 1], f32(T["gate_hi"][:]))
            nc.vector.tensor_tensor(T["vals"][:, :, :, 2], T["gate"][:], f32(T["gate_hi"][:]), ALU.subtract)
            dve.wait_ge(counted, 1)
            then(nc.vector.tensor_reduce(over[:, 0:1], ps[0:1, 0:E], AX.X, ALU.max))
            then(nc.vector.tensor_scalar(over[:, 1:2], over[:, 0:1], float(CAP) + 0.5, None, ALU.is_gt))
            then(nc.vector.tensor_copy(T["flag"][:], over[:, 1:2]))
            T["router_steps"] = done[0]

        @block.scalar
        def _(act):
            act.wait_ge(shifted, 1)
            nc.scalar.activation(z[:], z[:], ACT.Exp).then_inc(exped, 1)

        @block.tensor
        def _(pe):
            pe.wait_ge(consts, 5)
            pe.wait_ge(step, T["router_steps"] - 3)
            nc.tensor.matmul(ps[0:R, 0:E], T["ones_m"][:], cnt[:], start=True, stop=True).then_inc(counted, 1)


def threshold(nc, T):
    with ExitStack() as ctx:
        def sb(name, shape, dt=F32):
            return ctx.enter_context(nc.sbuf_tensor(name, shape, dt))

        def sem(name):
            return ctx.enter_context(nc.semaphore(name))

        low, cand, bit, add_i = sb("low", [R, E], I32), sb("cand", [R, E], I32), sb("bit", [R, E], I32), sb("add_i", [R, E], I32)
        take, cnt, quota = sb("take", [R, E]), sb("tcnt", [R, E]), sb("quota", [R, E])
        ge, above, tie, before = sb("ge", [R, E, NT]), sb("above", [R, E, NT]), sb("tie", [R, E, NT]), sb("before_t", [R, E, NT])
        ps = ctx.enter_context(nc.psum_tensor("th_ps", [128, 512], F32))
        step, part, counted, ranked = sem("th_step"), sem("th_part"), sem("th_counted"), sem("th_ranked")
        BITS = 30
        SETUP, PER = 2, 7
        block = ctx.enter_context(nc.Block())

        @block.vector
        def _(dve):
            def then(ins, at):
                ins.then_inc(step, 1)
                dve.wait_ge(step, at)

            then(nc.vector.memset(low[:], 0), 1)
            then(nc.vector.memset(bit[:], 1 << (BITS - 1)), 2)
            with dve.Fori(0, BITS) as i:
                at = SETUP + PER * i
                then(nc.vector.tensor_tensor(cand[:], low[:], bit[:], ALU.bitwise_or), at + 1)
                then(nc.vector.tensor_tensor(ge[:], T["gate"][:], each_token(cand[:].bitcast(F32)), ALU.is_ge), at + 2)
                then(nc.vector.tensor_tensor(ge[:], ge[:], T["has"][:], ALU.mult), at + 3)
                nc.vector.tensor_reduce(cnt[:], ge[:], AX.X, ALU.add).then_inc(part, 1)
                dve.wait_ge(counted, i + 1)
                then(nc.vector.tensor_scalar(take[:], ps[0:R, 0:E], float(CAP) - 0.5, None, ALU.is_gt), at + 4)
                then(nc.vector.tensor_tensor(add_i[:], take[:], bit[:], ALU.mult), at + 5)
                then(nc.vector.tensor_tensor(low[:], low[:], add_i[:], ALU.bitwise_or), at + 6)
                then(nc.vector.tensor_scalar(bit[:], bit[:], 1, None, ALU.logical_shift_right), at + 7)
            n = SETUP + PER * BITS
            least = each_token(low[:].bitcast(F32))
            then(nc.vector.tensor_tensor(above[:], T["gate"][:], least, ALU.is_gt), n + 1)
            then(nc.vector.tensor_tensor(above[:], above[:], T["has"][:], ALU.mult), n + 2)
            then(nc.vector.tensor_tensor(tie[:], T["gate"][:], least, ALU.is_equal), n + 3)
            then(nc.vector.tensor_tensor(tie[:], tie[:], T["has"][:], ALU.mult), n + 4)
            nc.vector.tensor_reduce(cnt[:], above[:], AX.X, ALU.add).then_inc(part, 1)
            dve.wait_ge(counted, BITS + 1)
            then(nc.vector.tensor_scalar(quota[:], ps[0:R, 0:E], -1.0, float(CAP), ALU.mult, ALU.add), n + 5)
            then(nc.vector.tensor_tensor_scan(flat(before[:]), flat(T["not_first"][:]), flat(tie[:]), 0.0, ALU.mult, ALU.add), n + 6)
            nc.vector.tensor_tensor(before[:], before[:], tie[:], ALU.subtract).then_inc(part, 1)
            dve.wait_ge(ranked, 1)
            then(nc.vector.tensor_tensor(ge[:], ps[0:R, 0:E * NT].rearrange("p (e t) -> p e t", e=E), each_token(quota[:]), ALU.is_lt), n + 7)
            then(nc.vector.tensor_tensor(tie[:], tie[:], ge[:], ALU.mult), n + 8)
            then(nc.vector.tensor_tensor(T["keep"][:], above[:], tie[:], ALU.add), n + 9)

        @block.tensor
        def _(pe):
            with pe.Fori(0, BITS + 1) as i:
                pe.wait_ge(part, i + 1)
                nc.tensor.matmul(ps[0:R, 0:E], T["ones_m"][:], cnt[:], start=True, stop=True).then_inc(counted, 1)
            pe.wait_ge(part, BITS + 2)
            nc.tensor.matmul(ps[0:R, 0:E * NT], T["after"][:], flat(tie[:]), start=True, stop=False)
            nc.tensor.matmul(ps[0:R, 0:E * NT], T["ones_m"][:], flat(before[:]), start=False, stop=True).then_inc(ranked, 1)

        @block.gpsimd
        def _(pool):
            pool.wait_ge(step, SETUP + PER * BITS + 9)

        @block.scalar
        def _(act):
            act.wait_ge(step, SETUP + PER * BITS + 9)

        @block.sync
        def _(sp):
            sp.wait_ge(step, SETUP + PER * BITS + 9)


STEPS = NBLK * FCH
PIECES = 4
WPAIRS = FCH // 2
QUART = NT // 4


def tile_rows(k, t):
    return min(128, CAP - (k * BLK + t) * 128)


def experts(nc, T, A):
    with ExitStack() as ctx:
        def sb(name, shape, dt=F32):
            return ctx.enter_context(nc.sbuf_tensor(name, shape, dt))

        def psum(name):
            return ctx.enter_context(nc.psum_tensor(name, [128, 512], F32))

        def sem(name):
            return ctx.enter_context(nc.semaphore(name))

        w1 = [sb(f"w1_{k}", [128, DCH, F], F32R) for k in ("hi", "lo")]
        w2 = [sb(f"w2_{k}", [128, FCH, D], F32R) for k in ("hi", "lo")]
        stage = sb("stage", [128, 2, PIECES, 512])
        xg, xT = sb("xg", [128, BLK, D]), [sb(f"xgT_{k}", [128, DCH, BLK * 128], F32R) for k in ("hi", "lo")]
        hT = [sb(f"hT_{k}", [128, 2, BLK * 128], F32R) for k in ("hi", "lo")]
        ys = sb("ys", [128, BLK, D])
        onehot, moves = sb("onehot", [R, 2, QUART, 128], F32R), sb("moves", [R, NT, CAPT, 4], F32R)
        eq_t, before, pos_i = sb("eq_t", [R, NT, CAPT]), sb("before", [R, E, NT]), sb("pos_i", [R, 2, E, NT], I32)
        slot, gsum = sb("slot", [128, CAPT, 4]), sb("gsum", [128, 3, CAPT])
        gid = [sb(f"gid_{k}", [128, CAPT], I32) for k in ("next", "now")]
        sid = [sb(f"sid_{k}", [128, CAPT], I32) for k in ("next", "now")]
        gate = [sb(f"slot_gate_{k}", [128, CAPT]) for k in ("next", "now")]
        psY, psH, psX, psI = [psum(f"psY{i}") for i in range(BLK)], [psum("psH0"), psum("psH1")], [psum("psX0"), psum("psX1")], psum("psI")

        w_in = [sem("w_in0"), sem("w_in1")]
        w_hi, w_lo = sem("w_split_hi"), sem("w_split_lo")
        gathered, scattered = sem("gathered"), sem("scattered")
        x_mm, x_hi, x_lo = sem("x_mm"), sem("x_hi"), sem("x_lo")
        h_mm, h_hi, h_lo = sem("h_mm"), sem("h_hi"), sem("h_lo")
        y_mm, y_done = sem("y_mm"), sem("y_done")
        marks, placed, prep = sem("marks"), sem("placed"), sem("prep")
        moves_done, onehot_done, slot_mm, slot_step, slots_next, slots_now = (
            sem("moves_done"), sem("onehot_done"), sem("slot_mm"), sem("slot_step"), sem("slots_next"), sem("slots_now"))
        eq_done, passed = sem("eq_done"), sem("passed")
        SLOT_STEPS = 5
        block = ctx.enter_context(nc.Block())

        def cols(k):
            return sum(tile_rows(k, t) for t in range(BLK))

        def refresh(k, f):
            if k == NBLK - 1 and f >= 2:
                return (f - 2) // 2, 2 * (f % 2)
            if k == 0 and f < 2:
                return WPAIRS - 1, 2 * f
            return None

        def piece(k, pair, j):
            if j < 2:
                return w1[k][:, 2 * j:2 * j + 2, pair * 256:(pair + 1) * 256]
            return w2[k][:, 2 * pair + j - 2, :]

        def staged(pair, j):
            s = stage[:, pair % 2, j, :]
            return s.rearrange("p (c f) -> p c f", c=2) if j < 2 else s

        @block.sync
        def _(sp):
            def load(e, pair, first):
                if not first:
                    sp.wait_ge(w_lo, PIECES * (WPAIRS * e + pair - 1))
                w = A["w1"][bass.ds(e, 1)].rearrange("o (c p) f -> p (o c) f", p=128)
                sp.dma_start(stage[:, pair % 2, 0:2, :].rearrange("p j (c f) -> p (j c) f", c=2),
                             w[:, :, pair * 256:(pair + 1) * 256]).then_inc(w_in[pair % 2], 16)
                w = A["w2"][bass.ds(e, 1)].rearrange("o (c p) n -> p (o c) n", p=128)
                sp.dma_start(stage[:, pair % 2, 2:4, :], w[:, 2 * pair:2 * pair + 2, :]).then_inc(w_in[pair % 2], 16)

            for pair in range(WPAIRS):
                load(0, pair, pair < 2)
            with sp.Fori(1, E) as e:
                for pair in range(WPAIRS):
                    load(e, pair, False)
            sp.wait_ge(scattered, 16 * CAPT * E)

        @block.gpsimd
        def _(pool):
            def gather(k, ids, sem, value):
                held(pool, passed, sem, value)
                for t in range(BLK):
                    n = tile_rows(k, t)
                    c = k * BLK + t
                    nc.gpsimd.indirect_dma_start(
                        out=xg[0:n, t, :], out_offset=None, in_=A["xn2"],
                        in_offset=bass.IndirectOffsetOnAxis(ap=ids[0:n, c:c + 1].bitcast(U32), axis=0)).then_inc(gathered, 16)

            def scatter(e, k):
                held(pool, passed, y_done, CAPT * e + BLK * (k + 1))
                for t in range(BLK):
                    n = tile_rows(k, t)
                    c = k * BLK + t
                    nc.gpsimd.indirect_dma_start(
                        out=A["out"], out_offset=bass.IndirectOffsetOnAxis(ap=sid[1][0:n, c:c + 1].bitcast(U32), axis=0),
                        in_=ys[0:n, t, :], in_offset=None, compute_op=ALU.add).then_inc(scattered, 16)

            def expert(e, nxt):
                pool.wait_ge(slots_now, e + 1)
                gather(1, gid[1], x_mm, DCH * (NBLK * e + 1))
                gather(2, gid[1], x_mm, DCH * (NBLK * e + 2))
                scatter(e, 0)
                if nxt:
                    pool.wait_ge(slots_next, e + 2)
                    gather(0, gid[0], x_mm, DCH * (NBLK * e + 3))
                scatter(e, 1)
                scatter(e, 2)

            gather(0, gid[0], slots_next, 1)
            expert(0, True)
            with pool.Fori(1, E - 1) as e:
                expert(e, True)
            expert(E - 1, False)

        @block.scalar
        def _(act):
            def split_w(e, pair, j):
                act.wait_ge(w_in[pair % 2], 32 * (WPAIRS // 2 * e + pair // 2 + 1))
                nc.scalar.activation(piece(0, pair, j), staged(pair, j), ACT.Copy).then_inc(w_hi, 1)

            def split_x(n, k):
                for c in range(DCH):
                    act.wait_ge(x_mm, DCH * n + c + 1)
                    nc.scalar.activation(xT[0][:, c, 0:cols(k)], psX[c % 2][:, 0:cols(k)], ACT.Copy).then_inc(x_hi, 1)

            def expert(e, nxt):
                for k in range(NBLK):
                    for f in range(FCH):
                        act.wait_ge(h_mm, STEPS * e + FCH * k + f + 1)
                        nc.scalar.activation(hT[0][:, f % 2, 0:cols(k)], psH[f % 2][:, 0:cols(k)], ACT.Relu).then_inc(h_hi, 1)
                        r = refresh(k, f)
                        if r and (k == 0 or nxt):
                            wait_unless_first(act, y_mm, STEPS * e if k == 0 else STEPS * e + FCH * k + 2 * r[0] + 2)
                            for j in (r[1], r[1] + 1):
                                split_w(e if k == 0 else e + 1, r[0], j)
                    if k < NBLK - 1 or nxt:
                        split_x(NBLK * e + k + 1, (k + 1) % NBLK)

            for pair in range(WPAIRS - 1):
                for j in range(PIECES):
                    split_w(0, pair, j)
            split_x(0, 0)
            expert(0, True)
            with act.Fori(1, E - 1) as e:
                expert(e, True)
            expert(E - 1, False)

        @block.vector
        def _(dve):
            def split_w(e, pair, j):
                dve.wait_ge(w_hi, PIECES * (WPAIRS * e + pair) + j + 1)
                nc.vector.tensor_tensor(piece(1, pair, j), staged(pair, j), f32(piece(0, pair, j)), ALU.subtract).then_inc(w_lo, 1)

            def split_x(n, k):
                for c in range(DCH):
                    dve.wait_ge(x_hi, DCH * n + c + 1)
                    nc.vector.tensor_tensor(xT[1][:, c, 0:cols(k)], psX[c % 2][:, 0:cols(k)], f32(xT[0][:, c, 0:cols(k)]),
                                            ALU.subtract).then_inc(x_lo, 1)

            def slot_moves(e):
                nc.vector.tensor_tensor(eq_t[:], T["iota_t"][:].unsqueeze(1).to_broadcast([R, NT, CAPT]),
                                        T["slot_tile"][:, bass.ds(e, 1), :].rearrange("p o t -> p (o t)").unsqueeze(2)
                                        .to_broadcast([R, NT, CAPT]), ALU.is_equal).then_inc(eq_done, 1)
                dve.wait_ge(eq_done, e + 1)
                nc.vector.tensor_tensor(moves[:], eq_t[:].unsqueeze(3).to_broadcast([R, NT, CAPT, 4]),
                                        T["vals"][:, bass.ds(e, 1), :, :].rearrange("p o t v -> p (o t) v").unsqueeze(2)
                                        .to_broadcast([R, NT, CAPT, 4]), ALU.mult).then_inc(moves_done, 1)

            def slot_onehot(e, q):
                if q >= 2:
                    dve.wait_ge(slot_mm, 4 * e + q - 1)
                nc.vector.tensor_tensor(onehot[:, q % 2], T["iota"][:].unsqueeze(1).to_broadcast([R, QUART, 128]),
                                        T["slot_row"][:, bass.ds(e, 1), q * QUART:(q + 1) * QUART]
                                        .rearrange("p o t -> p (o t)").unsqueeze(2).to_broadcast([R, QUART, 128]),
                                        ALU.is_equal).then_inc(onehot_done, 1)

            def slot_ids(e):
                def then(ins, at):
                    ins.then_inc(slot_step, 1)
                    dve.wait_ge(slot_step, SLOT_STEPS * e + at)

                dve.wait_ge(slot_mm, 4 * e + 4)
                then(nc.vector.tensor_copy(slot[:], psI[:, 0:CAPT * 4].rearrange("p (a v) -> p a v", v=4)), 1)
                nc.vector.tensor_copy(gid[0][:], slot[:, :, 0])
                nc.vector.tensor_tensor(gate[0][:], slot[:, :, 1], slot[:, :, 2], ALU.add)
                then(nc.vector.tensor_tensor(gsum[:, 0, :], slot[:, :, 3], T["dump"][:], ALU.mult), 2)
                then(nc.vector.tensor_tensor(gsum[:, 1, :], T["dump"][:], gsum[:, 0, :], ALU.subtract), 3)
                then(nc.vector.tensor_tensor(gsum[:, 2, :], gsum[:, 1, :], slot[:, :, 0], ALU.add), 4)
                then(nc.vector.tensor_copy(sid[0][:], gsum[:, 2, :]), 5)
                nc.vector.tensor_copy(slot[:, :, 0], slot[:, :, 3]).then_inc(slots_next, 1)

            def slots_take_over(e):
                dve.wait_ge(slots_next, e + 1)
                wait_unless_first(dve, scattered, 16 * CAPT * e)
                nc.vector.tensor_copy(gid[1][:], gid[0][:])
                nc.vector.tensor_copy(sid[1][:], sid[0][:])
                nc.vector.tensor_copy(gate[1][:], gate[0][:]).then_inc(slots_now, 1)

            def y_out(e, k):
                dve.wait_ge(y_mm, STEPS * e + FCH * (k + 1))
                dve.wait_ge(slots_now, e + 1)
                wait_unless_first(dve, scattered, 16 * (CAPT * e + BLK * k))
                for t in range(BLK):
                    n, c = tile_rows(k, t), k * BLK + t
                    nc.vector.tensor_scalar(ys[0:n, t, :], psY[t][0:n, :], gate[1][0:n, c:c + 1], None, ALU.mult).then_inc(y_done, 1)

            def expert(e, nxt):
                for k in range(NBLK):
                    for f in range(FCH):
                        n = cols(k)
                        dve.wait_ge(h_hi, STEPS * e + FCH * k + f + 1)
                        nc.vector.scalar_tensor_tensor(out=hT[1][:, f % 2, 0:n], in0=psH[f % 2][:, 0:n], scalar=0.0,
                                                       in1=f32(hT[0][:, f % 2, 0:n]), op0=ALU.max, op1=ALU.subtract).then_inc(h_lo, 1)
                        r = refresh(k, f)
                        if r and (k == 0 or nxt):
                            for j in (r[1], r[1] + 1):
                                split_w(e if k == 0 else e + 1, r[0], j)
                        if k == 0 and f == 8:
                            slots_take_over(e)
                        if k == 1 and nxt:
                            if f == 1:
                                slot_moves(e + 1)
                            if f in (3, 5, 7, 9):
                                slot_onehot(e + 1, (f - 3) // 2)
                            if f == 12:
                                slot_ids(e + 1)
                    if k < NBLK - 1 or nxt:
                        split_x(NBLK * e + k + 1, (k + 1) % NBLK)
                    y_out(e, k)

            nc.vector.tensor_tensor_scan(flat(before[:]), flat(T["not_first"][:]), flat(T["keep"][:]), 0.0,
                                         ALU.mult, ALU.add).then_inc(prep, 1)
            dve.wait_ge(prep, 1)
            nc.vector.tensor_tensor(before[:], before[:], T["keep"][:], ALU.subtract).then_inc(marks, 1)
            dve.wait_ge(placed, 1)
            pos = psI[0:R, 0:E * NT].rearrange("p (e t) -> p e t", e=E)
            nc.vector.tensor_copy(pos_i[:, 0], pos).then_inc(prep, 1)
            dve.wait_ge(prep, 2)
            nc.vector.tensor_scalar(pos_i[:, 1], pos_i[:, 0], 7, None, ALU.logical_shift_right).then_inc(prep, 1)
            dve.wait_ge(prep, 3)
            nc.vector.tensor_copy(T["slot_tile"][:], pos_i[:, 1])
            nc.vector.tensor_scalar(pos_i[:, 0], pos_i[:, 0], 127, None, ALU.bitwise_and).then_inc(prep, 1)
            dve.wait_ge(prep, 4)
            nc.vector.tensor_copy(before[:], pos_i[:, 0]).then_inc(prep, 1)
            dve.wait_ge(prep, 5)
            nc.vector.scalar_tensor_tensor(out=flat(before[:]), in0=flat(before[:]), scalar=1.0, in1=flat(T["keep"][:]),
                                           op0=ALU.add, op1=ALU.mult).then_inc(prep, 1)
            dve.wait_ge(prep, 6)
            nc.vector.tensor_scalar(T["slot_row"][:], before[:], -1.0, None, ALU.add).then_inc(prep, 1)
            dve.wait_ge(prep, 7)
            slot_moves(0)
            for q in range(4):
                slot_onehot(0, q)
            slot_ids(0)
            for pair in range(WPAIRS - 1):
                for j in range(PIECES):
                    split_w(0, pair, j)
            split_x(0, 0)
            expert(0, True)
            with dve.Fori(1, E - 1) as e:
                expert(e, True)
            expert(E - 1, False)

        @block.tensor
        def _(pe):
            def product(out, stationary, moving, chunks, first, last):
                for c in chunks:
                    for j, (a, b) in enumerate(((0, 0), (0, 1), (1, 0))):
                        mm = nc.tensor.matmul(out, stationary(a, c), moving(b, c), start=first and c == chunks[0] and j == 0,
                                              stop=last and c == chunks[-1] and j == 2, skip_group_check=True)
                return mm

            def turn(n, k, c):
                if c == 0:
                    pe.wait_ge(gathered, 16 * BLK * (n + 1))
                if c >= 2:
                    pe.wait_ge(x_lo, DCH * n + c - 1)
                at = 0
                for t in range(BLK):
                    m = tile_rows(k, t)
                    mm = nc.tensor.transpose(psX[c % 2][:, at:at + m], xg[0:m, t, c * 128:(c + 1) * 128], T["ident"][0:m, 0:m])
                    at += m
                mm.then_inc(x_mm, 1)

            def hidden(e, k, f):
                if f == 0:
                    pe.wait_ge(x_lo, DCH * (NBLK * e + k + 1))
                if k == 0 and f % 2 == 0:
                    pe.wait_ge(w_lo, PIECES * (WPAIRS * e + f // 2 + 1))
                if f >= 2 or k > 0:
                    pe.wait_ge(h_lo, STEPS * e + FCH * k + f - 1)
                n = cols(k)
                product(psH[f % 2][:, 0:n], lambda a, c: w1[a][:, c, f * 128:(f + 1) * 128], lambda b, c: xT[b][:, c, 0:n],
                        range(DCH), True, True).then_inc(h_mm, 1)

            def output(e, k, f):
                pe.wait_ge(h_lo, STEPS * e + FCH * k + f + 1)
                if f == 0:
                    wait_unless_first(pe, y_done, CAPT * e + BLK * k)
                for t in range(BLK):
                    m = tile_rows(k, t)
                    mm = product(psY[t][0:m, :], lambda a, c: hT[a][:, f % 2, t * 128:t * 128 + m], lambda b, c: w2[b][:, f, :],
                                 range(1), f == 0, f == FCH - 1)
                mm.then_inc(y_mm, 1)

            def slot_product(e, q):
                pe.wait_ge(onehot_done, 4 * e + q + 1)
                if q == 0:
                    pe.wait_ge(moves_done, e + 1)
                for t in range(QUART):
                    mm = nc.tensor.matmul(psI[:, 0:CAPT * 4], onehot[:, q % 2, t, :],
                                          moves[:, q * QUART + t].rearrange("p a v -> p (a v)"),
                                          start=q == 0 and t == 0, stop=q == 3 and t == QUART - 1, skip_group_check=True)
                mm.then_inc(slot_mm, 1)

            def expert(e, nxt):
                for k in range(NBLK):
                    more = k < NBLK - 1 or nxt
                    n, k2 = NBLK * e + k + 1, (k + 1) % NBLK
                    for f in range(FCH):
                        hidden(e, k, f)
                        if f == FCH - 1 and more:
                            turn(n, k2, 0)
                            turn(n, k2, 1)
                        if f:
                            output(e, k, f - 1)
                        if k == 1 and nxt and f in (4, 6, 8, 10):
                            slot_product(e + 1, (f - 4) // 2)
                    if more:
                        turn(n, k2, 2)
                        turn(n, k2, 3)
                    output(e, k, FCH - 1)

            pe.wait_ge(marks, 1)
            nc.tensor.matmul(psI[0:R, 0:E * NT], T["after"][:], flat(T["keep"][:]), start=True, stop=False)
            nc.tensor.matmul(psI[0:R, 0:E * NT], T["ones_m"][:], flat(before[:]), start=False, stop=True).then_inc(placed, 1)
            for q in range(4):
                slot_product(0, q)
            for c in range(DCH):
                turn(0, 0, c)
            expert(0, True)
            with pe.Fori(1, E - 1) as e:
                expert(e, True)
            expert(E - 1, False)


def persistent(nc, ctx):
    sb = lambda name, shape, dt=F32: ctx.enter_context(nc.sbuf_tensor(name, shape, dt))
    return {
        "ident": sb("ident", [128, 128]), "ones": sb("ones", [128, 1]), "mhalf": sb("mhalf", [128, TP]), "eps": sb("eps", [128, TP]),
        "flag": sb("flag", [1, 1], I32), "logits": sb("logits", [R, E, NT]),
    }


def routing(nc, ctx):
    sb = lambda name, shape, dt=F32: ctx.enter_context(nc.sbuf_tensor(name, shape, dt))
    return {
        "gate": sb("gate", [R, E, NT]), "has": sb("has", [R, E, NT]), "keep": sb("keep", [R, E, NT]),
        "gate_hi": sb("gate_hi", [R, E, NT], F32R), "vals": sb("vals", [R, E, NT, 4]),
        "slot_tile": sb("slot_tile", [R, E, NT]), "slot_row": sb("slot_row", [R, E, NT]), "not_first": sb("not_first", [R, E, NT]),
        "ones_m": sb("ones_m", [R, R]), "after": sb("after", [R, R]), "iota": sb("iota", [R, 128]),
        "iota_t": sb("iota_t", [R, CAPT]), "dump": sb("dump", [128, CAPT]),
    }


def flag_value(nc, T):
    return nc.values_load(T["flag"][0:1, 0:1], min_val=0, max_val=1, skip_runtime_bounds_check_because="it is a comparison's result")


def build(nc, x, ctx, mask, wq, wk, wv, wo, bo, wr, w1, w2, out):
    A = dict(x=x.rearrange("b s d -> (b s) d"), ctx=ctx, mask=mask.bitcast(U8).rearrange("(b k) -> b k", b=B), wq=wq, wk=wk, wv=wv, wo=wo,
             bo=bo, wr=wr, w1=w1, w2=w2, out=out)
    A["xn2"] = nc.dram_tensor("xn2_rows", [NTOK, D], F32, kind="Internal").ap()
    with ExitStack() as stack:
        T = persistent(nc, stack)
        with ExitStack() as att:
            sb = lambda name, shape, dt=F32: att.enter_context(nc.sbuf_tensor(name, shape, dt))
            T["w_hi"], T["w_lo"] = sb("w_hi", [128, 14, D], F32R), sb("w_lo", [128, 14, D], F32R)
            T["bias"], T["wr"] = sb("bias", [R, D]), sb("wr", [128, DCH, E])
            with nc.sbuf_tensor("zrow", [128, D], F32) as z:
                T["zrow"] = z
                preamble(nc, T, A)
            with nc.If(flag_value(nc, T) == 1):
                attention_short(nc, T, A)
            with nc.Else():
                attention_general(nc, T, A)
        T |= routing(nc, stack)
        router(nc, T)
        with nc.If(flag_value(nc, T) == 1):
            threshold(nc, T)
        experts(nc, T, A)


_INS = ["x", "ctx_768", "mask_BxS2_bk0", "L0_xattn_W_q", "L0_xattn_W_k", "L0_xattn_W_v", "L0_xattn_W_o", "L0_xattn_b_o",
        "L0_ffn_Wr", "L0_ffn_W1", "L0_ffn_W2"]


def kernel(**inputs):
    import numpy as _np
    import concourse.bacc as _bacc
    from concourse import mybir as _mybir
    from concourse.bass_utils import run_bass_kernel_spmd as _run

    nc = _bacc.Bacc("TRN2", target_bir_lowering=False, num_devices=1)
    arrays, args = {}, []
    for name in _INS:
        a = _np.ascontiguousarray(inputs[name])
        if a.dtype == _np.bool_:
            a = a.reshape(-1).view(_np.int32)
        arrays[f"in_{name}_dram"] = a
        args.append(nc.dram_tensor(f"in_{name}_dram", a.shape, _mybir.dt.from_np(a.dtype), kind="ExternalInput").ap())
    out = nc.dram_tensor("out_0_dram", (NTOK + NDUMP, D), _mybir.dt.float32, kind="ExternalOutput").ap()
    build(nc, *args, out)
    r = _run(nc, [arrays], core_ids=[0])
    return r.results[0]["out_0_dram"][:NTOK].reshape(B, S, D)
```

```python
from contextlib import ExitStack

import concourse.bass as bass
from concourse import mybir

F32 = mybir.dt.float32
F32R = mybir.dt.float32r
I32 = mybir.dt.int32
U32 = mybir.dt.uint32
U8 = mybir.dt.uint8
ALU = mybir.AluOpType
ACT = mybir.ActivationFunctionType
AX = mybir.AxisListType

B, S, D = 16, 224, 512
SK, DC = 750, 384
H, DH = 8, 64
E, F = 8, 2048
NTOK = B * S
CAP = 1120
R = 112
NT = NTOK // R
KC = 125
NKEY = 2 * KC
DCH, CCH = D // 128, DC // 128
HP = H // 2
EPS = 1e-5
BIG = 3.4028234663852886e38
SCALE = -(DH ** -0.5)
NPAIR = B // 2
TP = 4
CAPT = (CAP + 127) // 128
BLK = 3
NBLK = CAPT // BLK
FCH = F // 128
ZCOLS = 128
NDUMP = CAPT * 128


def f32(ap):
    return ap.bitcast(F32)


def wait_unless_first(engine, sem, value):
    if not isinstance(value, int) or value > 0:
        engine.wait_ge(sem, value)


def held(engine, passed, sem, value):
    engine.wait_ge(sem, value)
    engine.sem_inc(passed, 1)


def preamble(nc, T, A):
    with ExitStack() as ctx:
        mrow = ctx.enter_context(nc.sbuf_tensor("mask_rows", [B, SK], U8))
        m01 = ctx.enter_context(nc.sbuf_tensor("mask_any", [B, 4], F32))
        flag_ps = ctx.enter_context(nc.psum_tensor("flag_ps", [128, 512], F32))
        sem = lambda n: ctx.enter_context(nc.semaphore(n))
        b_in, mask_in, cleared, ident_done = sem("b_in"), sem("mask_in"), sem("cleared"), sem("ident_done")
        flag_step, flag_sum, filled = sem("flag_step"), sem("flag_sum"), sem("filled")
        block = ctx.enter_context(nc.Block())

        @block.sync
        def _(sp):
            sp.dma_start(mrow[:], A["mask"]).then_inc(mask_in, 16)
            load_front(sp, T, A, 0)
            sp.dma_start(T["bias"][:], A["bo"].rearrange("(a n) -> a n", a=1).partition_broadcast(R)).then_inc(b_in, 16)
            sp.dma_start(T["wr"][:], A["wr"].rearrange("(c p) n -> p c n", p=128)).then_inc(b_in, 16)
            sp.wait_ge(b_in, 32)

        @block.gpsimd
        def _(pool):
            pool.memset(T["ident"][:], 0.0).then_inc(cleared, 1)
            pool.wait_ge(cleared, 1)
            pool.affine_select(out=T["ident"][:], in_=T["ident"][:], compare_op=ALU.not_equal, fill=1.0, base=0,
                               pattern=[[-1, 128]], channel_multiplier=1).then_inc(ident_done, 1)
            pool.memset(T["mhalf"][:], -0.5).then_inc(ident_done, 1)
            pool.memset(T["eps"][:], EPS).then_inc(ident_done, 1)
            pool.memset(T["minus_one"][:], -1.0).then_inc(ident_done, 1)

        @block.vector
        def _(dve):
            nc.vector.memset(T["zrow"][:], 0.0).then_inc(filled, 1)
            nc.vector.memset(T["ones"][:], 1.0).then_inc(filled, 1)
            dve.wait_ge(mask_in, 16)
            nc.vector.tensor_reduce(m01[:, 0:1], mrow[:, 0:SK - NKEY], AX.X, ALU.max).then_inc(flag_step, 1)
            nc.vector.tensor_reduce(m01[:, 1:2], mrow[:, SK - NKEY:SK], AX.X, ALU.max).then_inc(flag_step, 1)
            dve.wait_ge(flag_step, 2)
            nc.vector.tensor_tensor(m01[:, 2:3], m01[:, 0:1], m01[:, 1:2], ALU.is_lt).then_inc(flag_step, 1)
            dve.wait_ge(flag_sum, 1)
            nc.vector.tensor_scalar(m01[0:1, 3:4], flag_ps[0:1, 0:1], float(B) - 0.5, None, ALU.is_gt).then_inc(flag_step, 1)
            dve.wait_ge(flag_step, 4)
            nc.vector.tensor_copy(T["flag"][:], m01[0:1, 3:4]).then_inc(flag_step, 1)
            dve.wait_ge(flag_step, 5)

        @block.tensor
        def _(pe):
            pe.wait_ge(flag_step, 3)
            pe.wait_ge(filled, 2)
            nc.tensor.matmul(flag_ps[0:1, 0:1], m01[:, 2:3], T["ones"][0:B, 0:1], start=True, stop=True).then_inc(flag_sum, 1)


def load_front(sp, T, A, p):
    x = A["x"].rearrange("(q t r) d -> q r t d", t=TP, r=R)[bass.ds(p, 1)]
    sp.dma_start(T["x_sb"][:], x.rearrange("o r t d -> (o r) t d")).then_inc(T["x_in"], 16)
    for b in range(2):
        c = A["ctx"].rearrange("(q b) (c r) d -> q b r c d", b=2, r=KC)[bass.ds(p, 1)]
        sp.dma_start(T["c_sb"][:, 2 * b:2 * b + 2, :],
                     c[:, b, :, SK // KC - 2:SK // KC, :].rearrange("o r c d -> (o r) c d")).then_inc(T["c_in"], 16)


def clear_dump_rows(sp, T, A):
    for a in range(CAPT):
        sp.dma_start(A["out"][NTOK + a * 128:NTOK + (a + 1) * 128, :].rearrange("r (a n) -> r a n", n=ZCOLS),
                     T["zrow"][:].unsqueeze(1).to_broadcast([128, D // ZCOLS, ZCOLS])).then_inc(T["dump_cleared"], 16)


PARTS = {"wv": (0, CCH), "wq": (CCH, DCH), "wk": (CCH + DCH, CCH), "wo": (2 * CCH + DCH, DCH)}
WCH = 2 * (CCH + DCH)


def chunks_before(name):
    return PARTS[name][0] + PARTS[name][1]


PRO_ORDER = [("fx", 0), ("fx", 1), ("fx", 2), ("fx", 3), ("fc", 0), ("fc", 1), ("fc", 2), ("v", 0), ("v", 1), ("q", 0), ("k", 0)]
ITER_ORDER = [("v", 2), ("v", 3), ("q", 1), ("k", 1), ("q", 2), ("k", 2), ("q", 3), ("k", 3),
              ("fx", 0), ("fx", 1), ("fx", 2), ("fx", 3), ("fc", 0), ("fc", 1), ("fc", 2), ("v", 0),
              ("wo", 0), ("wo", 1), ("wo", 2), ("wo", 3), ("v", 1),
              ("tt", 0), ("tt", 1), ("q", 0), ("tt", 2), ("tt", 3), ("k", 0), ("lg", 0)]
SPLIT_AT = {("fc", 0): "wv", ("fc", 2): "wq", ("v", 1): "wk"}
NPRO, NITER = len(PRO_ORDER), len(ITER_ORDER)
SPLIT = ("fx", "fc", "v", "q", "k")
HPRO = NPRO
HITER = sum(k in SPLIT for k, _ in ITER_ORDER)
LAST_ORDER = ITER_ORDER[:8] + [x for x in ITER_ORDER if x[0] in ("wo", "tt", "lg")]
NU = 16
LT = 3


FRONT = [("fx", 0), ("fx", 1), ("fx", 2), ("fx", 3), ("fc", 0), ("fc", 1), ("fc", 2)]


def steps(nxt):
    out = [("s", 0), ("s", 1), ("v", 2), ("v", 3), ("s", 2)]
    for u in range(3, NU):
        if u in (3, 6, 10):
            hp = {3: 1, 6: 2, 10: 3}[u]
            out += [("q", hp), ("k", hp)]
        out.append(("s", u))
        out.append(("t", u - LT))
        if u - LT - 1 >= 0:
            out.append(("o", u - LT - 1))
        if nxt and u > 10:
            out.append(FRONT[u - 11])
    out += [("t", 13), ("o", 12)] + FRONT[5:6] * nxt
    out += [("t", 14), ("o", 13)] + FRONT[6:7] * nxt
    out += [("t", 15), ("o", 14), ("o", 15)]
    out += [("v", 0)] * nxt + [("wo", 0), ("wo", 1), ("wo", 2), ("wo", 3)]
    out += [("v", 1)] * nxt + [("tt", 0), ("tt", 1)] + [("q", 0)] * nxt + [("tt", 2), ("tt", 3)]
    out += [("k", 0)] * nxt + [("lg", 0)]
    return out


def split_steps(nxt):
    out = steps(nxt)
    for n in range(len(out) - 1):
        if out[n][0] == "s" and out[n + 1][0] == "t":
            out[n], out[n + 1] = out[n + 1], out[n]
    return out


def attention_short(nc, T, A):
    with ExitStack() as ctx:
        def sb(name, shape, dt=F32):
            return ctx.enter_context(nc.sbuf_tensor(name, shape, dt))

        def psum(name):
            return ctx.enter_context(nc.psum_tensor(name, [128, 512], F32))

        def sem(name):
            return ctx.enter_context(nc.semaphore(name))

        x_sb, c_sb, x_in, c_in = T["x_sb"], T["c_sb"], T["x_in"], T["c_in"]
        m_sb, mb = sb("m_sb", [R, 2, NKEY], U8), sb("mask_bias", [R, 2, NKEY])
        xr = sb("x_res", [R, TP, D])
        xn2 = sb("xn2", [R, TP, D])
        xT = [sb(f"xT_{k}", [128, DCH, TP * R], F32R) for k in ("hi", "lo")]
        cT = [sb(f"cT_{k}", [128, CCH, TP * KC], F32R) for k in ("hi", "lo")]
        qz = [[sb(f"q{h}_{k}", [128, 2, TP * R], F32R) for k in ("hi", "lo")] for h in range(2)]
        kT = [sb(f"k_{k}", [128, 2, TP * KC], F32R) for k in ("hi", "lo")]
        v_sb = [sb(f"v_{k}", [KC, TP, HP, 192], F32R) for k in ("hi", "lo")]
        P = sb("probs", [R, 4, 2, NKEY])
        pT = [sb(f"pT_{k}", [KC, 2, 2 * S], F32R) for k in ("hi", "lo")]
        oT = [sb(f"oT_{k}", [128, HP, TP * R], F32R) for k in ("hi", "lo")]
        x2T = sb("x2T", [128, DCH, TP * R])
        w_raw = sb("w_raw", [128, 2, D])
        idle = x2T[:].rearrange("p c r -> p (c r)")
        ring_slots = [w_raw[:, 0, :], w_raw[:, 1, :]] + [idle[:, i * D:(i + 1) * D] for i in range(DCH * TP * R // D)]
        NS = len(ring_slots)
        lgT = sb("lgT", [E, TP * R])
        nmax, ssum, rsum = sb("nmax", [R, 4, 2]), sb("ssum", [R, 4, 2]), sb("rsum", [R, 4, 2])
        st1, mv1, rs1 = sb("st1", [R, TP, 6]), sb("mv1", [R, TP, 2]), sb("rs1", [R, TP])
        st2, mv2, rs2 = sb("st2", [R, TP, 6]), sb("mv2", [R, TP, 2]), sb("rs2", [R, TP])
        psS, psT = [psum("psS0"), psum("psS1")], [psum("psT0"), psum("psT1")]
        psO, psJ = [psum("psO0"), psum("psO1")], [psum("psJ0"), psum("psJ1")]

        m_in, xr_in = sem("m_in"), sem("xr_in")
        x2_out, xn2_out = sem("x2_out"), sem("xn2_out")
        proj_mm, proj_hi, proj_done = sem("proj_mm"), sem("proj_hi"), sem("proj_done")
        s_mm, masked, exped, recip, normed = sem("s_mm"), sem("masked"), sem("exped"), sem("recip"), sem("normed")
        t_mm, pt_hi, pt_lo = sem("t_mm"), sem("pt_hi"), sem("pt_lo")
        o_mm, o_hi, o_lo = sem("o_mm"), sem("o_hi"), sem("o_lo")
        st1_done, var1, eps1, rs1_done, xn_done = sem("st1_done"), sem("var1"), sem("eps1"), sem("rs1_done"), sem("xn_done")
        st2_done, var2, eps2, rs2_done, xn2_done = sem("st2_done"), sem("var2"), sem("eps2"), sem("rs2_done"), sem("xn2_done")
        biased, lg_copied, lg_t, mbias, zeros = sem("biased"), sem("lg_copied"), sem("lg_t"), sem("mbias"), sem("zeros")
        passed = sem("passed")
        w_in, w_hi, w_lo = [sem(f"w_in{i}") for i in range(NS)], sem("w_hi_done"), sem("w_lo_done")

        rows = lambda ap, p, t=TP: ap.rearrange("(q t r) d -> q r t d", t=t, r=R)[bass.ds(p, 1)].rearrange("o r t d -> (o r) t d")

        def m_row(p, b):
            v = A["mask"].rearrange("(q b) k -> q b k", b=2)[bass.ds(p, 1)]
            return v[:, b, SK - NKEY:SK].partition_broadcast(R)

        def order(nxt):
            return ITER_ORDER if nxt else LAST_ORDER

        def ring(p, nxt, kind, i):
            return PRO_ORDER.index((kind, i)) if p is None else order(nxt).index((kind, i)) + NPRO + NITER * p

        def bank(p, nxt, kind, i):
            if kind == "tt":
                return psT[i % 2]
            return psJ[(PRO_ORDER.index((kind, i)) if p is None else order(nxt).index((kind, i)) + NPRO) % 2]

        def hi_count(p, nxt, kind, i):
            if p is None:
                return PRO_ORDER.index((kind, i)) + 1
            return [x for x in order(nxt) if x[0] in SPLIT].index((kind, i)) + 1 + HPRO + HITER * p

        def v_half(src, h):
            return src[0:KC, 0:D].rearrange("p (a h d) -> p a h d", h=2, d=DH)[:, :, h, :]

        block = ctx.enter_context(nc.Block())

        @block.sync
        def _(sp):
            def load_mask(p):
                for b in range(2):
                    sp.dma_start(m_sb[:, b, :], m_row(p, b)).then_inc(m_in, 16)

            def iteration(p, nxt):
                sp.dma_start(xr[:], rows(A["x"], p)).then_inc(xr_in, 16)
                if nxt:
                    sp.wait_ge(proj_mm, PRO_ORDER.index(("fc", CCH - 1)) + 1 if isinstance(p, int) and p == 0 else ring(p - 1, True, "fc", 2) + 1)
                    load_front(sp, T, A, p + 1)
                    sp.wait_ge(mbias, p + 1)
                    load_mask(p + 1)
                    if isinstance(p, int) and p == 0:
                        clear_dump_rows(sp, T, A)
                sp.wait_ge(proj_done, ring(p, nxt, "wo", TP - 1) + 1)
                sp.dma_start(rows(A["out"][0:NTOK, :], p), xr[:]).then_inc(x2_out, 16)
                sp.wait_ge(xn2_done, TP * p + TP)
                sp.dma_start(rows(A["xn2"], p), xn2[:]).then_inc(xn2_out, 16)
                sp.wait_ge(x2_out, 16 * p + 16)
                held(sp, passed, xn2_out, 16 * p + 16)

            load_mask(0)
            for name, (at, n) in PARTS.items():
                for c in range(at, at + n):
                    if c >= NS:
                        sp.wait_ge(w_lo, c - NS + 1)
                    sp.dma_start(ring_slots[c % NS], A[name][(c - at) * 128:(c - at + 1) * 128, :]).then_inc(w_in[c % NS], 16)
            iteration(0, True)
            with sp.Fori(1, NPAIR - 1) as p:
                iteration(p, True)
            iteration(NPAIR - 1, False)

        @block.gpsimd
        def _(pool):
            def rstd(n, var_sem, mv, rs, e_sem, out_sem, cols):
                pool.wait_ge(var_sem, n)
                nc.gpsimd.tensor_tensor(rs, mv, T["eps"][0:R, 0:cols], ALU.add).then_inc(e_sem, 1)
                pool.wait_ge(e_sem, n)
                nc.gpsimd.tensor_tensor(rs, rs, T["mhalf"][0:R, 0:cols], ALU.pow).then_inc(out_sem, 1)

            def front_ln(n):
                rstd(n, var1, mv1[:, :, 1], rs1[:, :], eps1, rs1_done, TP)

            def iteration(p, nxt):
                pool.wait_ge(xr_in, 16 * p + 16)
                for t in range(TP):
                    nc.gpsimd.tensor_tensor(xr[:, t, :], xr[:, t, :], T["bias"][:], ALU.add).then_inc(biased, 1)
                for u in range(NU):
                    pool.wait_ge(exped, NU * p + u + 1)
                    nc.gpsimd.tensor_tensor(rsum[:, u % 4, :], ssum[:, u % 4, :], T["minus_one"][0:R, :], ALU.pow).then_inc(recip, 1)
                    pool.wait_ge(recip, NU * p + u + 1)
                    nc.gpsimd.tensor_tensor(P[:, u % 4], P[:, u % 4], rsum[:, u % 4, :].unsqueeze(2).to_broadcast([R, 2, NKEY]),
                                            ALU.mult).then_inc(normed, 1)
                    if nxt and u == TP:
                        front_ln(p + 2)
                for t in range(TP):
                    rstd(TP * p + t + 1, var2, mv2[:, t, 1:2], rs2[:, t:t + 1], eps2, rs2_done, 1)

            front_ln(1)
            for h in range(2):
                for k in range(2):
                    nc.gpsimd.memset(f32(qz[h][k][:]), 0.0).then_inc(zeros, 1)
            iteration(0, True)
            with pool.Fori(1, NPAIR - 1) as p:
                iteration(p, True)
            iteration(NPAIR - 1, False)

        @block.scalar
        def _(act):
            def split_hi(p, nxt, kind, i):
                act.wait_ge(proj_mm, ring(p, nxt, kind, i) + 1)
                src = bank(p, nxt, kind, i)
                if kind == "fx":
                    nc.scalar.activation(xT[0][:, i, :], src[:, 0:TP * R], ACT.Copy).then_inc(proj_hi, 1)
                elif kind == "fc":
                    nc.scalar.activation(cT[0][:, i, :], src[:, 0:TP * KC], ACT.Copy).then_inc(proj_hi, 1)
                elif kind == "v":
                    nc.scalar.activation(v_sb[0][:, i, :, 0:64], v_half(src, 0), ACT.Copy)
                    nc.scalar.activation(v_sb[0][:, i, :, 128:192], v_half(src, 1), ACT.Copy).then_inc(proj_hi, 1)
                elif kind == "q":
                    nc.scalar.activation(qz[0][0][0:64, i % 2, :], src[0:64, 0:TP * R], ACT.Copy)
                    nc.scalar.activation(qz[1][0][64:128, i % 2, :], src[64:128, 0:TP * R], ACT.Copy).then_inc(proj_hi, 1)
                else:
                    nc.scalar.activation(kT[0][:, i % 2, :], src[:, 0:TP * KC], ACT.Copy).then_inc(proj_hi, 1)

            def iteration(p, nxt):
                for kind, i in split_steps(nxt):
                    if kind in SPLIT:
                        split_hi(p, nxt, kind, i)
                    elif kind == "s":
                        act.wait_ge(masked, NU * p + i + 1)
                        for it in range(2):
                            e = nc.scalar.activation(P[:, i % 4, it, :], P[:, i % 4, it, :], ACT.Exp,
                                                     bias=nmax[:, i % 4, it:it + 1], scale=-1.0,
                                                     accum_out=ssum[:, i % 4, it:it + 1])
                        e.then_inc(exped, 1)
                    elif kind == "t":
                        act.wait_ge(t_mm, NU * p + i + 1)
                        nc.scalar.activation(pT[0][:, i % 2, :], psT[i % 2][0:KC, 0:2 * S], ACT.Copy).then_inc(pt_hi, 1)
                    elif kind == "o" and i % 2:
                        j, hp, b = i // 2, i // 4, (i // 2) % 2
                        act.wait_ge(o_mm, NU // 2 * p + j + 1)
                        nc.scalar.activation(oT[0][:, hp, b * S:(b + 1) * S], psO[j % 2][:, 0:S], ACT.Copy).then_inc(o_hi, 1)

            def split_weight(name):
                at, n = PARTS[name]
                for c in range(at, at + n):
                    act.wait_ge(w_in[c % NS], 16 * (c // NS + 1))
                    nc.scalar.activation(T["w_hi"][:, c, :], ring_slots[c % NS], ACT.Copy).then_inc(w_hi, 1)

            for kind, i in PRO_ORDER:
                if (kind, i) in SPLIT_AT:
                    split_weight(SPLIT_AT[kind, i])
                if kind == "v" and i == 0:
                    act.wait_ge(zeros, 6)
                split_hi(None, True, kind, i)
            split_weight("wo")
            iteration(0, True)
            with act.Fori(1, NPAIR - 1) as p:
                iteration(p, True)
            iteration(NPAIR - 1, False)

        @block.vector
        def _(dve):
            def split_lo(p, nxt, kind, i):
                dve.wait_ge(proj_hi, hi_count(p, nxt, kind, i))
                src = bank(p, nxt, kind, i)
                if kind == "fx":
                    a, h, o = src[:, 0:TP * R], xT[0][:, i, :], xT[1][:, i, :]
                elif kind == "fc":
                    a, h, o = src[:, 0:TP * KC], cT[0][:, i, :], cT[1][:, i, :]
                elif kind == "v":
                    nc.vector.tensor_tensor(v_sb[1][:, i, :, 0:64], v_half(src, 0), f32(v_sb[0][:, i, :, 0:64]), ALU.subtract)
                    a, h, o = v_half(src, 1), v_sb[0][:, i, :, 128:192], v_sb[1][:, i, :, 128:192]
                elif kind == "q":
                    nc.vector.tensor_tensor(qz[0][1][0:64, i % 2, :], src[0:64, 0:TP * R], f32(qz[0][0][0:64, i % 2, :]), ALU.subtract)
                    a, h, o = src[64:128, 0:TP * R], qz[1][0][64:128, i % 2, :], qz[1][1][64:128, i % 2, :]
                else:
                    a, h, o = src[:, 0:TP * KC], kT[0][:, i % 2, :], kT[1][:, i % 2, :]
                nc.vector.tensor_tensor(o, a, f32(h), ALU.subtract).then_inc(proj_done, 1)

            def front_stats(n, t):
                if t == 0:
                    dve.wait_ge(x_in, 16 * n)
                s = nc.vector.bn_stats(st1[:, t, :], x_sb[:, t, :])
                if t == TP - 1:
                    s.then_inc(st1_done, 1)

            def front_aggr(n):
                held(dve, passed, st1_done, n)
                for t in range(TP):
                    s = nc.vector.bn_aggr(mv1[:, t, :], st1[:, t, :])
                s.then_inc(var1, 1)

            def front_apply(n, t):
                if t == 0:
                    dve.wait_ge(rs1_done, n)
                s = nc.vector.tensor_scalar(x_sb[:, t, :], x_sb[:, t, :], mv1[:, t, 0:1], rs1[:, t:t + 1],
                                            ALU.subtract, ALU.mult)
                if t == TP - 1:
                    s.then_inc(xn_done, 1)

            def mask_bias(n):
                dve.wait_ge(m_in, 32 * n)
                nc.vector.tensor_scalar(mb[:], m_sb[:], 1.0, BIG, ALU.subtract, ALU.mult).then_inc(mbias, 1)
                dve.wait_ge(mbias, n)

            def tail_stats(p, nxt, t):
                dve.wait_ge(proj_mm, ring(p, nxt, "wo", t) + 1)
                if t == 0:
                    dve.wait_ge(biased, TP * p + TP)
                nc.vector.tensor_tensor(xr[:, t, :], bank(p, nxt, "wo", t)[0:R, :], xr[:, t, :], ALU.add).then_inc(proj_done, 1)
                dve.wait_ge(proj_done, ring(p, nxt, "wo", t) + 1)
                nc.vector.bn_stats(st2[:, t, :], xr[:, t, :]).then_inc(st2_done, 1)
                held(dve, passed, st2_done, TP * p + t + 1)
                nc.vector.bn_aggr(mv2[:, t, :], st2[:, t, :]).then_inc(var2, 1)

            def tail_apply(p, t):
                dve.wait_ge(rs2_done, TP * p + t + 1)
                nc.vector.tensor_scalar(xn2[:, t, :], xr[:, t, :], mv2[:, t, 0:1], rs2[:, t:t + 1],
                                        ALU.subtract, ALU.mult).then_inc(xn2_done, 1)

            def iteration(p, nxt):
                for kind, i in steps(nxt):
                    if kind in SPLIT:
                        split_lo(p, nxt, kind, i)
                        if nxt and (kind, i) == ("v", 1):
                            tail_apply(p, TP - 1)
                        if nxt and (kind, i) == ("k", 0):
                            mask_bias(p + 2)
                    elif kind == "s":
                        held(dve, passed, s_mm, NU * p + i + 1)
                        b = (i // 2) % 2
                        for it in range(2):
                            s = nc.vector.tensor_tensor_reduce(
                                out=P[:, i % 4, it, :], in0=psS[i % 2][0:R, it * NKEY:(it + 1) * NKEY], in1=mb[:, b, :],
                                scale=SCALE, scalar=BIG, op0=ALU.add, op1=ALU.min, accum_out=nmax[:, i % 4, it:it + 1])
                        s.then_inc(masked, 1)
                        if nxt and 1 <= i <= TP:
                            front_stats(p + 2, i - 1)
                        if nxt and i == TP + 1:
                            front_aggr(p + 2)
                        if nxt and TP + 3 <= i <= 2 * TP + 2:
                            front_apply(p + 2, i - TP - 3)
                    elif kind == "t":
                        dve.wait_ge(pt_hi, NU * p + i + 1)
                        nc.vector.tensor_tensor(pT[1][:, i % 2, :], psT[i % 2][0:KC, 0:2 * S], f32(pT[0][:, i % 2, :]),
                                                ALU.subtract).then_inc(pt_lo, 1)
                    elif kind == "o" and i % 2:
                        j, hp, b = i // 2, i // 4, (i // 2) % 2
                        dve.wait_ge(o_hi, NU // 2 * p + j + 1)
                        nc.vector.tensor_tensor(oT[1][:, hp, b * S:(b + 1) * S], psO[j % 2][:, 0:S],
                                                f32(oT[0][:, hp, b * S:(b + 1) * S]), ALU.subtract).then_inc(o_lo, 1)
                    elif kind == "wo":
                        tail_stats(p, nxt, i)
                        if i:
                            tail_apply(p, i - 1)
                        if i == TP - 1 and not nxt:
                            tail_apply(p, i)
                    elif kind == "tt":
                        dve.wait_ge(proj_mm, ring(p, nxt, "tt", i) + 1)
                        src = bank(p, nxt, "tt", i)[:, 0:DCH * R].rearrange("p (c r) -> p c r", c=DCH)
                        nc.vector.tensor_copy(x2T[:, :, i * R:(i + 1) * R], src).then_inc(proj_done, 1)
                    elif kind == "lg":
                        dve.wait_ge(proj_mm, ring(p, nxt, "lg", 0) + 1)
                        src = bank(p, nxt, "lg", 0)
                        nc.vector.tensor_copy(lgT[:], src[0:E, 0:TP * R]).then_inc(lg_copied, 1)
                        dve.wait_ge(lg_t, p + 1)
                        nc.vector.tensor_copy(
                            T["logits"][:, :, bass.ds(p * TP, TP)].rearrange("p e t -> p t e"),
                            src[0:R, TP * R:TP * R + TP * E].rearrange("p (t e) -> p t e", e=E)).then_inc(proj_done, 1)

            for t in range(TP):
                front_stats(1, t)
            front_aggr(1)
            for t in range(TP):
                front_apply(1, t)
            for k in range(2):
                nc.vector.memset(f32(v_sb[k][:, :, :, 64:128]), 0.0).then_inc(zeros, 1)
            mask_bias(1)
            def split_weight(name):
                at, n = PARTS[name]
                for c in range(at, at + n):
                    dve.wait_ge(w_hi, c + 1)
                    nc.vector.tensor_tensor(T["w_lo"][:, c, :], ring_slots[c % NS], f32(T["w_hi"][:, c, :]),
                                            ALU.subtract).then_inc(w_lo, 1)

            for kind, i in PRO_ORDER:
                if (kind, i) in SPLIT_AT:
                    split_weight(SPLIT_AT[kind, i])
                split_lo(None, True, kind, i)
            split_weight("wo")
            iteration(0, True)
            with dve.Fori(1, NPAIR - 1) as p:
                iteration(p, True)
            iteration(NPAIR - 1, False)

        @block.tensor
        def _(pe):
            ident = T["ident"]

            def product(out, stationary, moving, n, first=True, last=True):
                for c in range(n):
                    for j, (a, b) in enumerate(((0, 0), (0, 1), (1, 0))):
                        mm = nc.tensor.matmul(out, stationary(a, c), moving(b, c), start=first and c == 0 and j == 0,
                                              stop=last and c == n - 1 and j == 2, skip_group_check=True)
                return mm

            def w(name):
                at, n = PARTS[name]
                return [T["w_hi"][:, at:at + n, :], T["w_lo"][:, at:at + n, :]]

            wq, wk, wv, wo = w("wq"), w("wk"), w("wv"), w("wo")

            def proj(p, nxt, kind, i, n):
                at = ring(p, nxt, kind, i)
                out = bank(p, nxt, kind, i)
                if (p is not None or at >= 2) and (kind, i) not in (("tt", 0), ("tt", 1)):
                    last = {("q", 0): ("wo", TP - 1), ("k", 0): ("v", 1), ("tt", 2): ("tt", 0),
                            ("tt", 3): ("tt", 1)}.get((kind, i)) if p is not None else None
                    pe.wait_ge(proj_done, ring(p, nxt, *last) + 1 if last else at - 1)
                if p is None and (kind, i) in (("v", 0), ("q", 0), ("k", 0)):
                    pe.wait_ge(w_lo, chunks_before("w" + kind))
                if isinstance(p, int) and p == 0 and (kind, i) == ("wo", 0):
                    pe.wait_ge(w_lo, WCH)
                if kind == "fx":
                    pe.wait_ge(xn_done, n)
                    for t in range(TP):
                        mm = nc.tensor.transpose(out[:, t * R:(t + 1) * R], x_sb[:, t, i * 128:(i + 1) * 128], ident[0:R, 0:R])
                elif kind == "fc":
                    pe.wait_ge(c_in, 32 * n)
                    for j in range(TP):
                        mm = nc.tensor.transpose(out[:, j * KC:(j + 1) * KC], c_sb[:, j, i * 128:(i + 1) * 128], ident[0:KC, 0:KC])
                elif kind == "v":
                    if i == 0:
                        pe.wait_ge(proj_done, ring(p, nxt, "fc", CCH - 1) + 1)
                    mm = product(out[0:KC, :], lambda k, c: cT[k][:, c, i * KC:(i + 1) * KC], lambda k, c: wv[k][:, c, :], CCH)
                elif kind == "q":
                    mm = product(out[:, 0:TP * R], lambda k, c: wq[k][:, c, i * 128:(i + 1) * 128], lambda k, c: xT[k][:, c, :], DCH)
                elif kind == "k":
                    mm = product(out[:, 0:TP * KC], lambda k, c: wk[k][:, c, i * 128:(i + 1) * 128], lambda k, c: cT[k][:, c, :], CCH)
                elif kind == "wo":
                    if i == 0:
                        pe.wait_ge(o_lo, NU // 2 * p + NU // 2)
                    mm = product(out[0:R, :], lambda k, c: oT[k][:, c, i * R:(i + 1) * R], lambda k, c: wo[k][:, c, :], HP)
                elif kind == "tt":
                    pe.wait_ge(xn2_done, TP * p + i + 1)
                    for c in range(DCH):
                        mm = nc.tensor.transpose(out[:, c * R:(c + 1) * R], xn2[:, i, c * 128:(c + 1) * 128], ident[0:R, 0:R])
                else:
                    pe.wait_ge(proj_done, ring(p, nxt, "tt", TP - 1) + 1)
                    for c in range(DCH):
                        mm = nc.tensor.matmul(out[0:E, 0:TP * R], T["wr"][:, c, :], x2T[:, c, :], start=c == 0, stop=c == DCH - 1)
                mm.then_inc(proj_mm, 1)
                if kind == "lg":
                    held(pe, passed, lg_copied, p + 1)
                    for t in range(TP):
                        mm = nc.tensor.transpose(out[0:R, TP * R + t * E:TP * R + (t + 1) * E], lgT[:, t * R:(t + 1) * R], ident[0:E, 0:E])
                    mm.then_inc(lg_t, 1)

            def iteration(p, nxt):
                for kind, i in steps(nxt):
                    hp, b, h = i // 4, (i // 2) % 2, i % 2
                    if kind == "s":
                        if i == 0:
                            first = isinstance(p, int) and p == 0
                            pe.wait_ge(proj_done, (ring(None, True, "k", 0) if first else ring(p - 1, True, "k", 0)) + 1)
                        elif i % 4 == 0:
                            pe.wait_ge(proj_done, ring(p, nxt, "k", hp) + 1)
                        if i >= 2:
                            pe.wait_ge(masked, NU * p + i - 1)
                        for it in range(2):
                            at = b * S + it * R
                            mm = product(psS[i % 2][0:R, it * NKEY:(it + 1) * NKEY],
                                         lambda k, c: qz[h][k][:, hp % 2, at:at + R],
                                         lambda k, c: kT[k][:, hp % 2, b * NKEY:(b + 1) * NKEY], 1)
                        mm.then_inc(s_mm, 1)
                    elif kind == "t":
                        pe.wait_ge(normed, NU * p + i + 1)
                        if i >= 2:
                            pe.wait_ge(pt_lo, NU * p + i - 1)
                        for c in range(2):
                            for it in range(2):
                                mm = nc.tensor.transpose(psT[i % 2][0:KC, c * S + it * R:c * S + (it + 1) * R],
                                                         P[:, i % 4, it, c * KC:(c + 1) * KC], ident[0:R, 0:R])
                        mm.then_inc(t_mm, 1)
                    elif kind == "o":
                        pe.wait_ge(pt_lo, NU * p + i + 1)
                        if i == 2:
                            pe.wait_ge(proj_done, ring(p, nxt, "v", 3) + 1)
                        if i % 2 == 0 and i >= 4:
                            pe.wait_ge(o_lo, NU // 2 * p + i // 2 - 1)
                        mm = product(psO[(i // 2) % 2][:, 0:S], lambda k, c: v_sb[k][:, 2 * b + c, hp, h * DH:h * DH + 128],
                                     lambda k, c: pT[k][:, i % 2, c * S:(c + 1) * S], 2, first=h == 0, last=h == 1)
                        if h:
                            mm.then_inc(o_mm, 1)
                    else:
                        proj(p, nxt, kind, i, p + 2)

            for kind, i in PRO_ORDER:
                if kind == "v" and i == 0:
                    pe.wait_ge(zeros, 6)
                proj(None, True, kind, i, 1)
            iteration(0, True)
            with pe.Fori(1, NPAIR - 1) as p:
                iteration(p, True)
            iteration(NPAIR - 1, False)


GSTEPS = 5 + 2 * H + 2


def general_order():
    out = [("xT", c, 0) for c in range(DCH)] + [("cT", c, 0) for c in range(CCH)] + [("v", j, 0) for j in range(SK // KC)]
    for h in range(H):
        out += [("q", h, 0), ("k", h, 0)]
        for it in range(2):
            out += [("s", h, it), ("pT", h, it), ("o", h, it)]
    for it in range(2):
        out += [("oT", 0, it), ("wo", 0, it), ("x2T", 0, it), ("lg", 0, it)]
    return out


def attention_general(nc, T, A):
    with ExitStack() as ctx:
        def sb(name, shape, dt=F32):
            return ctx.enter_context(nc.sbuf_tensor(f"g_{name}", shape, dt))

        def sem(name):
            return ctx.enter_context(nc.semaphore(f"g_{name}"))

        NK, HALF = SK // KC, SK // 2
        ORDER = general_order()
        w = sb("w", [128, WCH, D])
        wq, wk, wv, wo = (w[:, PARTS[name][0]:chunks_before(name), :] for name in ("wq", "wk", "wv", "wo"))
        x_sb, xr, xn2, c_sb = sb("x", [R, 2, D]), sb("xr", [R, 2, D]), sb("xn2", [R, 2, D]), sb("c", [KC, NK, DC])
        m_sb, mb, P = sb("m", [R, SK], U8), sb("mask_bias", [R, SK]), sb("probs", [R, SK])
        xT, cT = sb("xT", [128, DCH, 2 * R]), sb("cT", [128, CCH, SK])
        qT, kT, v_sb = sb("qT", [DH, 2 * R]), sb("kT", [DH, SK]), sb("v", [KC, NK, D])
        pT, o_sb, oT, x2T = sb("pT", [KC, NK, R]), sb("o", [R, 2, D]), sb("oT", [128, DCH, R]), sb("x2T", [128, DCH, R])
        nmin, ssum = sb("nmin", [R, 3]), sb("ssum", [R, 2])
        st, mv, rs = sb("st", [R, 2, 6]), sb("mv", [R, 2, 2]), sb("rs", [R, 2])
        ps = [ctx.enter_context(nc.psum_tensor(f"g_ps{i}", [128, 512], F32)) for i in range(2)]
        w_in, x_in, c_in, m_in, xr_in, out_done, xn2_out = (sem("w_in"), sem("x_in"), sem("c_in"), sem("m_in"), sem("xr_in"),
                                                            sem("out_done"), sem("xn2_out"))
        made, taken, step, masked, exped, normed = sem("made"), sem("taken"), sem("step"), sem("masked"), sem("exped"), sem("normed")
        passed = sem("passed")
        var, eps, rs_done, xn_done, x2_done, xn2_done = (sem("var"), sem("eps"), sem("rs_done"), sem("xn_done"), sem("x2_done"),
                                                         sem("xn2_done"))
        N = len(ORDER)
        TAKEN = N - 2
        block = ctx.enter_context(nc.Block())

        @block.sync
        def _(sp):
            sp.wait_ge(T["x_in"], 16)
            sp.wait_ge(T["c_in"], 32)
            for name, (at, n) in PARTS.items():
                sp.dma_start(w[:, at:at + n, :], A[name].rearrange("(c p) n -> p c n", p=128)).then_inc(w_in, 16)
            clear_dump_rows(sp, T, A)
            with sp.Fori(0, B) as b:
                rows = lambda ap: ap.rearrange("(q t r) d -> q r t d", t=2, r=R)[bass.ds(b, 1)].rearrange("o r t d -> (o r) t d")
                sp.wait_ge(taken, 1 + TAKEN * b)
                sp.dma_start(x_sb[:], rows(A["x"])).then_inc(x_in, 16)
                sp.dma_start(xr[:], rows(A["x"])).then_inc(xr_in, 16)
                sp.dma_start(c_sb[:], A["ctx"].rearrange("q (c r) d -> q r c d", r=KC)[bass.ds(b, 1)]
                             .rearrange("o r c d -> (o r) c d")).then_inc(c_in, 16)
                sp.dma_start(m_sb[:], A["mask"][bass.ds(b, 1), :].partition_broadcast(R)).then_inc(m_in, 16)
                sp.wait_ge(x2_done, 2 * b + 2)
                sp.dma_start(rows(A["out"][0:NTOK, :]), xr[:]).then_inc(out_done, 16)
                sp.wait_ge(xn2_done, 2 * b + 2)
                sp.dma_start(rows(A["xn2"]), xn2[:]).then_inc(xn2_out, 16)
                sp.wait_ge(out_done, 16 * b + 16)
                held(sp, passed, xn2_out, 16 * b + 16)

        @block.gpsimd
        def _(pool):
            def rstd(n, cols, v, r):
                pool.wait_ge(var, n)
                nc.gpsimd.tensor_tensor(r, v, T["eps"][0:R, 0:cols], ALU.add).then_inc(eps, 1)
                pool.wait_ge(eps, n)
                nc.gpsimd.tensor_tensor(r, r, T["mhalf"][0:R, 0:cols], ALU.pow).then_inc(rs_done, 1)

            with pool.Fori(0, B) as b:
                rstd(3 * b + 1, 2, mv[:, :, 1], rs[:, :])
                for it in range(2):
                    rstd(3 * b + it + 2, 1, mv[:, it, 1:2], rs[:, it:it + 1])

        @block.scalar
        def _(act):
            with act.Fori(0, B) as b:
                for i in range(2 * H):
                    act.wait_ge(masked, 2 * H * b + i + 1)
                    nc.scalar.activation(P[:], P[:], ACT.Exp, bias=nmin[:, 2:3], scale=-1.0, accum_out=ssum[:, 0:1]).then_inc(exped, 1)

        @block.vector
        def _(dve):
            dve.sem_inc(taken, 1)
            with dve.Fori(0, B) as b:
                done = [0]

                def then(ins):
                    done[0] += 1
                    ins.then_inc(step, 1)
                    held(dve, passed, step, GSTEPS * b + done[0])

                dve.wait_ge(m_in, 16 * b + 16)
                then(nc.vector.tensor_scalar(mb[:], m_sb[:], 1.0, BIG, ALU.subtract, ALU.mult))
                dve.wait_ge(x_in, 16 * b + 16)
                for it in range(2):
                    then(nc.vector.bn_stats(st[:, it, :], x_sb[:, it, :]))
                nc.vector.bn_aggr(mv[:, 0, :], st[:, 0, :])
                nc.vector.bn_aggr(mv[:, 1, :], st[:, 1, :]).then_inc(var, 1)
                dve.wait_ge(rs_done, 3 * b + 1)
                for it in range(2):
                    nc.vector.tensor_scalar(x_sb[:, it, :], x_sb[:, it, :], mv[:, it, 0:1], rs[:, it:it + 1],
                                            ALU.subtract, ALU.mult).then_inc(xn_done, 1)
                dve.wait_ge(xr_in, 16 * b + 16)
                for it in range(2):
                    then(nc.vector.tensor_tensor(xr[:, it, :], xr[:, it, :], T["bias"][:], ALU.add))
                for n, (kind, i, it) in enumerate(ORDER):
                    if kind == "s":
                        held(dve, passed, made, N * b + n + 1)
                    else:
                        dve.wait_ge(made, N * b + n + 1)
                    if kind == "xT":
                        last = nc.vector.tensor_copy(xT[:, i, :], ps[0][:, 0:2 * R])
                    elif kind == "cT":
                        nc.vector.tensor_copy(cT[:, i, 0:HALF], ps[0][:, 0:HALF])
                        last = nc.vector.tensor_copy(cT[:, i, HALF:SK], ps[1][:, 0:HALF])
                    elif kind == "v":
                        last = nc.vector.tensor_copy(v_sb[:, i, :], ps[0][0:KC, :])
                    elif kind == "q":
                        last = nc.vector.tensor_copy(qT[:], ps[0][0:DH, 0:2 * R])
                    elif kind == "k":
                        nc.vector.tensor_copy(kT[:, 0:HALF], ps[0][0:DH, 0:HALF])
                        last = nc.vector.tensor_copy(kT[:, HALF:SK], ps[1][0:DH, 0:HALF])
                    elif kind == "s":
                        for k in range(2):
                            s = nc.vector.tensor_tensor_reduce(
                                out=P[:, k * HALF:(k + 1) * HALF], in0=ps[k][0:R, 0:HALF], in1=mb[:, k * HALF:(k + 1) * HALF],
                                scale=SCALE, scalar=BIG, op0=ALU.add, op1=ALU.min, accum_out=nmin[:, k:k + 1])
                        then(s)
                        nc.vector.tensor_tensor(nmin[:, 2:3], nmin[:, 0:1], nmin[:, 1:2], ALU.min).then_inc(masked, 1)
                        dve.wait_ge(exped, 2 * H * b + 2 * i + it + 1)
                        nc.vector.reciprocal(ssum[:, 1:2], ssum[:, 0:1]).then_inc(normed, 1)
                        dve.wait_ge(normed, 2 * H * b + 2 * i + it + 1)
                        last = nc.vector.tensor_scalar(P[:], P[:], ssum[:, 1:2], None, ALU.mult)
                    elif kind == "pT":
                        for k in range(2):
                            last = nc.vector.tensor_copy(pT[:, k * NK // 2:(k + 1) * NK // 2, :],
                                                         ps[k][0:KC, 0:NK // 2 * R].rearrange("p (c r) -> p c r", r=R))
                    elif kind == "o":
                        last = nc.vector.tensor_copy(o_sb[:, it, i * DH:(i + 1) * DH], ps[0][0:R, 0:DH])
                    elif kind == "oT":
                        last = nc.vector.tensor_copy(oT[:], ps[0][:, 0:DCH * R].rearrange("p (c r) -> p c r", r=R))
                    elif kind == "wo":
                        nc.vector.tensor_tensor(xr[:, it, :], ps[0][0:R, :], xr[:, it, :], ALU.add).then_inc(x2_done, 1)
                        dve.wait_ge(x2_done, 2 * b + it + 1)
                        then(nc.vector.bn_stats(st[:, it, :], xr[:, it, :]))
                        nc.vector.bn_aggr(mv[:, it, :], st[:, it, :]).then_inc(var, 1)
                        dve.wait_ge(rs_done, 3 * b + it + 2)
                        nc.vector.tensor_scalar(xn2[:, it, :], xr[:, it, :], mv[:, it, 0:1], rs[:, it:it + 1],
                                                ALU.subtract, ALU.mult).then_inc(xn2_done, 1)
                    elif kind == "x2T":
                        last = nc.vector.tensor_copy(x2T[:], ps[0][:, 0:DCH * R].rearrange("p (c r) -> p c r", r=R))
                    else:
                        last = nc.vector.tensor_copy(T["logits"][:, :, bass.ds(2 * b + it, 1)].rearrange("p e o -> p (e o)"),
                                                     ps[0][0:R, 0:E])
                    if kind != "wo":
                        last.then_inc(taken, 1)
                assert done[0] == GSTEPS

        @block.tensor
        def _(pe):
            ident = T["ident"]

            def product(out, stationary, moving, n):
                for c in range(n):
                    mm = nc.tensor.matmul(out, stationary(c), moving(c), start=c == 0, stop=c == n - 1)
                return mm

            pe.wait_ge(w_in, 64)
            with pe.Fori(0, B) as b:
                for n, (kind, i, it) in enumerate(ORDER):
                    pe.wait_ge(taken, 1 + TAKEN * b + sum(k != "wo" for k, _, _ in ORDER[:n]))
                    if kind == "x2T":
                        pe.wait_ge(xn2_done, 2 * b + it + 1)
                    mine = slice(it * R, (it + 1) * R)
                    if kind == "xT":
                        pe.wait_ge(xn_done, 2 * b + 2)
                        for t in range(2):
                            mm = nc.tensor.transpose(ps[0][:, t * R:(t + 1) * R], x_sb[:, t, i * 128:(i + 1) * 128], ident[0:R, 0:R])
                    elif kind == "cT":
                        pe.wait_ge(c_in, 16 * b + 16)
                        for j in range(NK):
                            at = j % (NK // 2) * KC
                            mm = nc.tensor.transpose(ps[j // (NK // 2)][:, at:at + KC], c_sb[:, j, i * 128:(i + 1) * 128],
                                                     ident[0:KC, 0:KC])
                    elif kind == "v":
                        mm = product(ps[0][0:KC, :], lambda c: cT[:, c, i * KC:(i + 1) * KC], lambda c: wv[:, c, :], CCH)
                    elif kind == "q":
                        mm = product(ps[0][0:DH, 0:2 * R], lambda c: wq[:, c, i * DH:(i + 1) * DH], lambda c: xT[:, c, :], DCH)
                    elif kind == "k":
                        for k in range(2):
                            mm = product(ps[k][0:DH, 0:HALF], lambda c: wk[:, c, i * DH:(i + 1) * DH],
                                         lambda c: cT[:, c, k * HALF:(k + 1) * HALF], CCH)
                    elif kind == "s":
                        for k in range(2):
                            mm = nc.tensor.matmul(ps[k][0:R, 0:HALF], qT[:, mine], kT[:, k * HALF:(k + 1) * HALF], start=True, stop=True)
                    elif kind == "pT":
                        for j in range(NK):
                            at = j % (NK // 2) * R
                            mm = nc.tensor.transpose(ps[j // (NK // 2)][0:KC, at:at + R], P[:, j * KC:(j + 1) * KC], ident[0:R, 0:R])
                    elif kind == "o":
                        mm = product(ps[0][0:R, 0:DH], lambda c: pT[:, c, :], lambda c: v_sb[:, c, i * DH:(i + 1) * DH], NK)
                    elif kind in ("oT", "x2T"):
                        src = o_sb if kind == "oT" else xn2
                        for c in range(DCH):
                            mm = nc.tensor.transpose(ps[0][:, c * R:(c + 1) * R], src[:, it, c * 128:(c + 1) * 128], ident[0:R, 0:R])
                    elif kind == "wo":
                        mm = product(ps[0][0:R, :], lambda c: oT[:, c, :], lambda c: wo[:, c, :], DCH)
                    else:
                        mm = product(ps[0][0:R, 0:E], lambda c: x2T[:, c, :], lambda c: T["wr"][:, c, :], DCH)
                    mm.then_inc(made, 1)


def over_experts(ap):
    return ap.rearrange("p e t -> p t e")


def each_expert(ap):
    return ap.unsqueeze(1).to_broadcast([R, E, NT])


def each_token(ap):
    return ap.unsqueeze(2).to_broadcast([R, E, NT])


def flat(ap):
    return ap.rearrange("p e t -> p (e t)")


STEPS = NBLK * FCH
PIECES = 4
WPAIRS = FCH // 2
QUART = NT // 4
EARLY = 2
EARLY_LO = 1
POOL_PAIRS = 4
BEFORE = 5


def piece(T, k, pair, j):
    if j < 2:
        return T["w1"][k][:, 2 * j:2 * j + 2, pair * 256:(pair + 1) * 256]
    return T["w2"][k][:, 2 * pair + j - 2, :]


def staged(T, pair, j):
    s = T["stage"][:, pair % 2, j, :]
    return s.rearrange("p (c f) -> p c f", c=2) if j < 2 else s


def load_pair(sp, T, A, e, pair):
    w = A["w1"][bass.ds(e, 1)].rearrange("o (c p) f -> p (o c) f", p=128)
    sp.dma_start(T["stage"][:, pair % 2, 0:2, :].rearrange("p j (c f) -> p (j c) f", c=2),
                 w[:, :, pair * 256:(pair + 1) * 256]).then_inc(T["w_in"][pair % 2], 16)
    w = A["w2"][bass.ds(e, 1)].rearrange("o (c p) n -> p (o c) n", p=128)
    sp.dma_start(T["stage"][:, pair % 2, 2:4, :], w[:, 2 * pair:2 * pair + 2, :]).then_inc(T["w_in"][pair % 2], 16)


def split_pair_hi(act, nc, T, e, pair, j):
    act.wait_ge(T["w_in"][pair % 2], 32 * (WPAIRS // 2 * e + pair // 2 + 1))
    nc.scalar.activation(piece(T, 0, pair, j), staged(T, pair, j), ACT.Copy).then_inc(T["w_hi_done"], 1)


def split_pair_lo(engine, T, e, pair, j):
    engine.wait_ge(T["w_hi_done"], PIECES * (WPAIRS * e + pair) + j + 1)
    engine.tensor_tensor(piece(T, 1, pair, j), staged(T, pair, j), f32(piece(T, 0, pair, j)), ALU.subtract).then_inc(T["w_lo_done"], 1)


def router(nc, T, A):
    with ExitStack() as ctx:
        def sb(name, shape, dt=F32):
            return ctx.enter_context(nc.sbuf_tensor(name, shape, dt))

        def sem(name):
            return ctx.enter_context(nc.semaphore(name))

        z, probs, rest = sb("z", [R, E, NT]), sb("router_probs", [R, E, NT]), sb("rest", [R, E, NT])
        eq, rank, sel = sb("eq", [R, E, NT]), sb("rank", [R, E, NT]), sb("sel", [R, 2, E, NT])
        rank_i, id_i = sb("rank_i", [R, E, NT], I32), sb("id_i", [R, NT], I32)
        iota_i, iota_t, dump_i = sb("iota_i", [R, 128], I32), sb("iota_t_i", [R, CAPT], I32), sb("dump_i", [128, CAPT], I32)
        red, cnt, over = sb("red", [R, 4, NT]), sb("cnt", [R, E]), sb("over", [1, 2])
        more = sb("more_f", [1, E, NBLK])
        ps = ctx.enter_context(nc.psum_tensor("count_ps", [128, 512], F32))
        iotas, consts, step, shifted, exped, counted = (sem("iotas"), sem("consts"), sem("step"), sem("shifted"),
                                                        sem("exped"), sem("counted"))
        tallied = sem("tallied")
        block = ctx.enter_context(nc.Block())

        @block.sync
        def _(sp):
            for pair in range(EARLY):
                load_pair(sp, T, A, 0, pair)
            sp.wait_ge(T["dump_cleared"], 16 * CAPT)

        @block.gpsimd
        def _(pool):
            nc.gpsimd.iota(rank_i[:], pattern=[[-1, E], [0, NT]], base=E, channel_multiplier=0).then_inc(iotas, 1)
            nc.gpsimd.iota(id_i[:], pattern=[[R, NT]], base=0, channel_multiplier=1).then_inc(iotas, 1)
            nc.gpsimd.iota(iota_i[:], pattern=[[1, 128]], base=0, channel_multiplier=0).then_inc(iotas, 1)
            nc.gpsimd.iota(iota_t[:], pattern=[[1, CAPT]], base=0, channel_multiplier=0).then_inc(iotas, 1)
            nc.gpsimd.iota(dump_i[:], pattern=[[128, CAPT]], base=NTOK, channel_multiplier=1).then_inc(iotas, 1)
            nc.gpsimd.memset(T["ones_m"][:], 1.0).then_inc(consts, 1)
            nc.gpsimd.memset(T["after"][:], 1.0).then_inc(consts, 1)
            nc.gpsimd.memset(T["not_first"][:], 1.0).then_inc(consts, 1)
            pool.wait_ge(consts, 3)
            nc.gpsimd.affine_select(out=T["after"][:], in_=T["after"][:], compare_op=ALU.is_gt, fill=0.0, base=0,
                                    pattern=[[1, R]], channel_multiplier=-1).then_inc(consts, 1)
            nc.gpsimd.memset(T["not_first"][:, :, 0:1], 0.0).then_inc(consts, 1)
            for pair in range(EARLY_LO):
                for j in range(PIECES):
                    split_pair_lo(nc.gpsimd, T, 0, pair, j)

        @block.vector
        def _(dve):
            done = [0]

            def then(ins):
                done[0] += 1
                ins.then_inc(step, 1)
                dve.wait_ge(step, done[0])

            logits = T["logits"]
            dve.wait_ge(iotas, 5)
            nc.vector.tensor_copy(rank[:], rank_i[:])
            nc.vector.tensor_copy(T["iota"][:], iota_i[:])
            nc.vector.tensor_copy(T["iota_t"][:], iota_t[:])
            nc.vector.tensor_copy(T["dump"][:], dump_i[:])
            nc.vector.tensor_copy(T["vals"][:, :, :, 0], each_expert(id_i[:]))
            nc.vector.memset(T["vals"][:, :, :, 3], 1.0)
            then(nc.vector.tensor_reduce(red[:, 0, :], over_experts(logits[:]), AX.X, ALU.max))
            nc.vector.tensor_tensor(z[:], logits[:], each_expert(red[:, 0, :]), ALU.subtract).then_inc(shifted, 1)
            dve.wait_ge(exped, 1)
            then(nc.vector.tensor_reduce(red[:, 1, :], over_experts(z[:]), AX.X, ALU.add))
            then(nc.vector.reciprocal(red[:, 2, :], red[:, 1, :]))
            then(nc.vector.tensor_tensor(probs[:], z[:], each_expert(red[:, 2, :]), ALU.mult))
            src = probs
            for k in range(2):
                then(nc.vector.tensor_reduce(red[:, 0, :], over_experts(src[:]), AX.X, ALU.max))
                then(nc.vector.tensor_tensor(eq[:], src[:], each_expert(red[:, 0, :]), ALU.is_equal))
                then(nc.vector.tensor_tensor(eq[:], eq[:], rank[:], ALU.mult))
                then(nc.vector.tensor_reduce(red[:, 3, :], over_experts(eq[:]), AX.X, ALU.max))
                then(nc.vector.tensor_tensor(sel[:, k], rank[:], each_expert(red[:, 3, :]), ALU.is_equal))
                if k == 0:
                    then(nc.vector.scalar_tensor_tensor(out=flat(rest[:]), in0=flat(sel[:, 0]), scalar=-2.0, in1=flat(probs[:]),
                                                        op0=ALU.mult, op1=ALU.add))
                    src = rest
            then(nc.vector.tensor_tensor(T["has"][:], sel[:, 0], sel[:, 1], ALU.add))
            then(nc.vector.tensor_tensor(T["gate"][:], probs[:], T["has"][:], ALU.mult))
            nc.vector.tensor_copy(T["gate_hi"][:], T["gate"][:])
            nc.vector.tensor_copy(T["keep"][:], T["has"][:])
            nc.vector.tensor_reduce(cnt[:], T["has"][:], AX.X, ALU.add).then_inc(tallied, 1)
            dve.wait_ge(tallied, 1)
            nc.vector.tensor_copy(T["vals"][:, :, :, 1], f32(T["gate_hi"][:]))
            nc.vector.tensor_tensor(T["vals"][:, :, :, 2], T["gate"][:], f32(T["gate_hi"][:]), ALU.subtract)
            dve.wait_ge(counted, 1)
            for k in range(NBLK):
                nc.vector.tensor_scalar(more[:, :, k], ps[0:1, 0:E], TILES[k][-1] * 128 + 0.5, None, ALU.is_gt)
            then(nc.vector.tensor_reduce(over[:, 0:1], ps[0:1, 0:E], AX.X, ALU.max))
            then(nc.vector.tensor_scalar(over[:, 1:2], over[:, 0:1], float(CAP) + 0.5, None, ALU.is_gt))
            nc.vector.tensor_copy(T["more"][:], more[:].rearrange("p e k -> p (e k)"))
            then(nc.vector.tensor_copy(T["flag"][:], over[:, 1:2]))

        @block.scalar
        def _(act):
            act.wait_ge(shifted, 1)
            nc.scalar.activation(z[:], z[:], ACT.Exp).then_inc(exped, 1)
            for pair in range(EARLY):
                for j in range(PIECES):
                    split_pair_hi(act, nc, T, 0, pair, j)

        @block.tensor
        def _(pe):
            pe.wait_ge(consts, 5)
            pe.wait_ge(tallied, 1)
            nc.tensor.matmul(ps[0:R, 0:E], T["ones_m"][:], cnt[:], start=True, stop=True).then_inc(counted, 1)


def threshold(nc, T):
    with ExitStack() as ctx:
        def sb(name, shape, dt=F32):
            return ctx.enter_context(nc.sbuf_tensor(name, shape, dt))

        def sem(name):
            return ctx.enter_context(nc.semaphore(name))

        low, cand, bit, add_i = sb("low", [R, E], I32), sb("cand", [R, E], I32), sb("bit", [R, E], I32), sb("add_i", [R, E], I32)
        take, cnt, quota = sb("take", [R, E]), sb("tcnt", [R, E]), sb("quota", [R, E])
        ge, above, tie, before = sb("ge", [R, E, NT]), sb("above", [R, E, NT]), sb("tie", [R, E, NT]), sb("before_t", [R, E, NT])
        ps = ctx.enter_context(nc.psum_tensor("th_ps", [128, 512], F32))
        step, part, counted, ranked = sem("th_step"), sem("th_part"), sem("th_counted"), sem("th_ranked")
        BITS = 30
        SETUP, PER = 2, 7
        block = ctx.enter_context(nc.Block())

        @block.vector
        def _(dve):
            def then(ins, at):
                ins.then_inc(step, 1)
                dve.wait_ge(step, at)

            then(nc.vector.memset(low[:], 0), 1)
            then(nc.vector.memset(bit[:], 1 << (BITS - 1)), 2)
            with dve.Fori(0, BITS) as i:
                at = SETUP + PER * i
                then(nc.vector.tensor_tensor(cand[:], low[:], bit[:], ALU.bitwise_or), at + 1)
                then(nc.vector.tensor_tensor(ge[:], T["gate"][:], each_token(cand[:].bitcast(F32)), ALU.is_ge), at + 2)
                then(nc.vector.tensor_tensor(ge[:], ge[:], T["has"][:], ALU.mult), at + 3)
                nc.vector.tensor_reduce(cnt[:], ge[:], AX.X, ALU.add).then_inc(part, 1)
                dve.wait_ge(counted, i + 1)
                then(nc.vector.tensor_scalar(take[:], ps[0:R, 0:E], float(CAP) - 0.5, None, ALU.is_gt), at + 4)
                then(nc.vector.tensor_tensor(add_i[:], take[:], bit[:], ALU.mult), at + 5)
                then(nc.vector.tensor_tensor(low[:], low[:], add_i[:], ALU.bitwise_or), at + 6)
                then(nc.vector.tensor_scalar(bit[:], bit[:], 1, None, ALU.logical_shift_right), at + 7)
            n = SETUP + PER * BITS
            least = each_token(low[:].bitcast(F32))
            then(nc.vector.tensor_tensor(above[:], T["gate"][:], least, ALU.is_gt), n + 1)
            then(nc.vector.tensor_tensor(above[:], above[:], T["has"][:], ALU.mult), n + 2)
            then(nc.vector.tensor_tensor(tie[:], T["gate"][:], least, ALU.is_equal), n + 3)
            then(nc.vector.tensor_tensor(tie[:], tie[:], T["has"][:], ALU.mult), n + 4)
            nc.vector.tensor_reduce(cnt[:], above[:], AX.X, ALU.add).then_inc(part, 1)
            dve.wait_ge(counted, BITS + 1)
            then(nc.vector.tensor_scalar(quota[:], ps[0:R, 0:E], -1.0, float(CAP), ALU.mult, ALU.add), n + 5)
            then(nc.vector.tensor_tensor_scan(flat(before[:]), flat(T["not_first"][:]), flat(tie[:]), 0.0, ALU.mult, ALU.add), n + 6)
            nc.vector.tensor_tensor(before[:], before[:], tie[:], ALU.subtract).then_inc(part, 1)
            dve.wait_ge(ranked, 1)
            then(nc.vector.tensor_tensor(ge[:], ps[0:R, 0:E * NT].rearrange("p (e t) -> p e t", e=E), each_token(quota[:]), ALU.is_lt), n + 7)
            then(nc.vector.tensor_tensor(tie[:], tie[:], ge[:], ALU.mult), n + 8)
            then(nc.vector.tensor_tensor(T["keep"][:], above[:], tie[:], ALU.add), n + 9)

        @block.tensor
        def _(pe):
            with pe.Fori(0, BITS + 1) as i:
                pe.wait_ge(part, i + 1)
                nc.tensor.matmul(ps[0:R, 0:E], T["ones_m"][:], cnt[:], start=True, stop=True).then_inc(counted, 1)
            pe.wait_ge(part, BITS + 2)
            nc.tensor.matmul(ps[0:R, 0:E * NT], T["after"][:], flat(tie[:]), start=True, stop=False)
            nc.tensor.matmul(ps[0:R, 0:E * NT], T["ones_m"][:], flat(before[:]), start=False, stop=True).then_inc(ranked, 1)

        @block.gpsimd
        def _(pool):
            pool.wait_ge(step, SETUP + PER * BITS + 9)

        @block.scalar
        def _(act):
            act.wait_ge(step, SETUP + PER * BITS + 9)

        @block.sync
        def _(sp):
            sp.wait_ge(step, SETUP + PER * BITS + 9)




TILES = ((0, 1, 8), (2, 3, 7), (4, 5, 6))


def tile_rows(k, t):
    return min(128, CAP - TILES[k][t] * 128)


def experts(nc, T, A):
    with ExitStack() as ctx:
        def sb(name, shape, dt=F32):
            return ctx.enter_context(nc.sbuf_tensor(name, shape, dt))

        def psum(name):
            return ctx.enter_context(nc.psum_tensor(name, [128, 512], F32))

        def sem(name):
            return ctx.enter_context(nc.semaphore(name))

        w1, w2 = T["w1"], T["w2"]
        xg, xT = sb("xg", [128, BLK, D]), [sb(f"xgT_{k}", [128, DCH, BLK * 128], F32R) for k in ("hi", "lo")]
        hT = [sb(f"hT_{k}", [128, 2, BLK * 128], F32R) for k in ("hi", "lo")]
        ys = sb("ys", [128, BLK, D])
        onehot, moves = sb("onehot", [R, 2, QUART, 128], F32R), sb("moves", [R, NT, CAPT, 4], F32R)
        eq_t, before, pos_i = sb("eq_t", [R, NT, CAPT]), sb("before", [R, E, NT]), sb("pos_i", [R, 2, E, NT], I32)
        slot, gsum = sb("slot", [128, CAPT, 4]), sb("gsum", [128, 3, CAPT])
        gid = [sb(f"gid_{k}", [128, CAPT], I32) for k in ("next", "now")]
        sid = [sb(f"sid_{k}", [128, CAPT], I32) for k in ("next", "now")]
        gate = [sb(f"slot_gate_{k}", [128, CAPT]) for k in ("next", "now")]
        psY, psH, psX, psI = [psum(f"psY{i}") for i in range(BLK)], [psum("psH0"), psum("psH1")], [psum("psX0"), psum("psX1")], psum("psI")

        gathered, scattered = sem("gathered"), sem("scattered")
        x_mm, x_hi, x_lo = sem("x_mm"), sem("x_hi"), sem("x_lo")
        h_mm, h_hi, h_lo = sem("h_mm"), sem("h_hi"), sem("h_lo")
        y_mm, y_done = sem("y_mm"), sem("y_done")
        marks, placed, prep = sem("marks"), sem("placed"), sem("prep")
        moves_done, onehot_done, slot_mm, slot_step, slots_next, slots_now = (
            sem("moves_done"), sem("onehot_done"), sem("slot_mm"), sem("slot_step"), sem("slots_next"), sem("slots_now"))
        eq_done, passed, cleared = sem("eq_done"), sem("passed"), sem("y_cleared")
        SLOT_STEPS = 5
        block = ctx.enter_context(nc.Block())

        def cols(k):
            return sum(tile_rows(k, t) for t in range(BLK))

        def refresh(e, k, f):
            if isinstance(e, int) and e == 0 and k == 0:
                return (BEFORE + f // 2, 2 * (f % 2)) if f < 2 * (WPAIRS - BEFORE) else None
            if k == NBLK - 1 and f >= 2:
                return (f - 2) // 2, 2 * (f % 2)
            if k == 0 and f < 2:
                return WPAIRS - 1, 2 * f
            return None

        @block.sync
        def _(sp):
            def load(e, pair):
                sp.wait_ge(T["w_lo_done"], PIECES * (WPAIRS * e + pair - 1))
                load_pair(sp, T, A, e, pair)

            for pair in range(EARLY, WPAIRS):
                load(0, pair)
            with sp.Fori(1, E) as e:
                for pair in range(WPAIRS):
                    load(e, pair)
            sp.wait_ge(scattered, 16 * CAPT * E)

        @block.gpsimd
        def _(pool):
            def gather(k, ids, sem, value):
                held(pool, passed, sem, value)
                for t in range(BLK):
                    n = tile_rows(k, t)
                    c = TILES[k][t]
                    nc.gpsimd.indirect_dma_start(
                        out=xg[0:n, t, :], out_offset=None, in_=A["xn2"],
                        in_offset=bass.IndirectOffsetOnAxis(ap=ids[0:n, c:c + 1].bitcast(U32), axis=0)).then_inc(gathered, 16)

            def scatter(e, k):
                held(pool, passed, y_done, CAPT * e + BLK * (k + 1))
                for t in range(BLK):
                    n = tile_rows(k, t)
                    c = TILES[k][t]
                    nc.gpsimd.indirect_dma_start(
                        out=A["out"], out_offset=bass.IndirectOffsetOnAxis(ap=sid[1][0:n, c:c + 1].bitcast(U32), axis=0),
                        in_=ys[0:n, t, :], in_offset=None, compute_op=ALU.add).then_inc(scattered, 16)

            def expert(e, nxt):
                pool.wait_ge(slots_now, e + 1)
                gather(1, gid[1], x_mm, DCH * (NBLK * e + 1))
                gather(2, gid[1], x_mm, DCH * (NBLK * e + 2))
                scatter(e, 0)
                if nxt:
                    pool.wait_ge(slots_next, e + 2)
                    gather(0, gid[0], x_mm, DCH * (NBLK * e + 3))
                scatter(e, 1)
                scatter(e, 2)

            for pair in range(EARLY_LO, POOL_PAIRS):
                for j in range(PIECES):
                    split_pair_lo(nc.gpsimd, T, 0, pair, j)
            gather(0, gid[0], slots_next, 1)
            expert(0, True)
            with pool.Fori(1, E - 1) as e:
                expert(e, True)
            expert(E - 1, False)

        @block.scalar
        def _(act):
            def split_x(n, k):
                for c in range(DCH):
                    act.wait_ge(x_mm, DCH * n + c + 1)
                    nc.scalar.activation(xT[0][:, c, 0:cols(k)], psX[c % 2][:, 0:cols(k)], ACT.Copy).then_inc(x_hi, 1)

            def expert(e, nxt):
                for k in range(NBLK):
                    for f in range(FCH):
                        act.wait_ge(h_mm, STEPS * e + FCH * k + f + 1)
                        nc.scalar.activation(hT[0][:, f % 2, 0:cols(k)], psH[f % 2][:, 0:cols(k)], ACT.Relu).then_inc(h_hi, 1)
                        r = refresh(e, k, f)
                        if r and (k == 0 or nxt):
                            wait_unless_first(act, y_mm, STEPS * e if k == 0 else STEPS * e + FCH * k + 2 * r[0] + 2)
                            for j in (r[1], r[1] + 1):
                                split_pair_hi(act, nc, T, e if k == 0 else e + 1, r[0], j)
                    if k < NBLK - 1 or nxt:
                        split_x(NBLK * e + k + 1, (k + 1) % NBLK)

            for pair in range(EARLY, BEFORE):
                for j in range(PIECES):
                    split_pair_hi(act, nc, T, 0, pair, j)
            split_x(0, 0)
            expert(0, True)
            with act.Fori(1, E - 1) as e:
                expert(e, True)
            expert(E - 1, False)

        @block.vector
        def _(dve):
            def split_x(n, k):
                for c in range(DCH):
                    dve.wait_ge(x_hi, DCH * n + c + 1)
                    nc.vector.tensor_tensor(xT[1][:, c, 0:cols(k)], psX[c % 2][:, 0:cols(k)], f32(xT[0][:, c, 0:cols(k)]),
                                            ALU.subtract).then_inc(x_lo, 1)

            def slot_moves(e):
                nc.vector.tensor_tensor(eq_t[:], T["iota_t"][:].unsqueeze(1).to_broadcast([R, NT, CAPT]),
                                        T["slot_tile"][:, bass.ds(e, 1), :].rearrange("p o t -> p (o t)").unsqueeze(2)
                                        .to_broadcast([R, NT, CAPT]), ALU.is_equal).then_inc(eq_done, 1)
                dve.wait_ge(eq_done, e + 1)
                nc.vector.tensor_tensor(moves[:], eq_t[:].unsqueeze(3).to_broadcast([R, NT, CAPT, 4]),
                                        T["vals"][:, bass.ds(e, 1), :, :].rearrange("p o t v -> p (o t) v").unsqueeze(2)
                                        .to_broadcast([R, NT, CAPT, 4]), ALU.mult).then_inc(moves_done, 1)

            def slot_onehot(e, q):
                if q >= 2:
                    dve.wait_ge(slot_mm, 4 * e + q - 1)
                nc.vector.tensor_tensor(onehot[:, q % 2], T["iota"][:].unsqueeze(1).to_broadcast([R, QUART, 128]),
                                        T["slot_row"][:, bass.ds(e, 1), q * QUART:(q + 1) * QUART]
                                        .rearrange("p o t -> p (o t)").unsqueeze(2).to_broadcast([R, QUART, 128]),
                                        ALU.is_equal).then_inc(onehot_done, 1)

            def slot_ids(e):
                def then(ins, at):
                    ins.then_inc(slot_step, 1)
                    dve.wait_ge(slot_step, SLOT_STEPS * e + at)

                dve.wait_ge(slot_mm, 4 * e + 4)
                then(nc.vector.tensor_copy(slot[:], psI[:, 0:CAPT * 4].rearrange("p (a v) -> p a v", v=4)), 1)
                nc.vector.tensor_copy(gid[0][:], slot[:, :, 0])
                nc.vector.tensor_tensor(gate[0][:], slot[:, :, 1], slot[:, :, 2], ALU.add)
                then(nc.vector.tensor_tensor(gsum[:, 0, :], slot[:, :, 3], T["dump"][:], ALU.mult), 2)
                then(nc.vector.tensor_tensor(gsum[:, 1, :], T["dump"][:], gsum[:, 0, :], ALU.subtract), 3)
                then(nc.vector.tensor_tensor(gsum[:, 2, :], gsum[:, 1, :], slot[:, :, 0], ALU.add), 4)
                then(nc.vector.tensor_copy(sid[0][:], gsum[:, 2, :]), 5)
                nc.vector.tensor_copy(slot[:, :, 0], slot[:, :, 3]).then_inc(slots_next, 1)

            def slots_take_over(e):
                dve.wait_ge(slots_next, e + 1)
                wait_unless_first(dve, scattered, 16 * CAPT * e)
                nc.vector.tensor_copy(gid[1][:], gid[0][:])
                nc.vector.tensor_copy(sid[1][:], sid[0][:])
                nc.vector.tensor_copy(gate[1][:], gate[0][:]).then_inc(slots_now, 1)

            def y_out(e, k):
                dve.wait_ge(y_mm, STEPS * e + FCH * (k + 1))
                dve.wait_ge(slots_now, e + 1)
                wait_unless_first(dve, scattered, 16 * (CAPT * e + BLK * k))
                for t in range(BLK):
                    n, c = tile_rows(k, t), TILES[k][t]
                    nc.vector.tensor_scalar(ys[0:n, t, :], psY[t][0:n, :], gate[1][0:n, c:c + 1], None, ALU.mult).then_inc(y_done, 1)

            def expert(e, nxt):
                for k in range(NBLK):
                    for f in range(FCH):
                        n = cols(k)
                        dve.wait_ge(h_hi, STEPS * e + FCH * k + f + 1)
                        nc.vector.scalar_tensor_tensor(out=hT[1][:, f % 2, 0:n], in0=psH[f % 2][:, 0:n], scalar=0.0,
                                                       in1=f32(hT[0][:, f % 2, 0:n]), op0=ALU.max, op1=ALU.subtract).then_inc(h_lo, 1)
                        r = refresh(e, k, f)
                        if r and (k == 0 or nxt):
                            for j in (r[1], r[1] + 1):
                                split_pair_lo(nc.vector, T, e if k == 0 else e + 1, r[0], j)
                        if k == 0 and f == 8:
                            slots_take_over(e)
                        if k == 1 and nxt:
                            if f == 1:
                                slot_moves(e + 1)
                            if f in (3, 5, 7, 9):
                                slot_onehot(e + 1, (f - 3) // 2)
                            if f == 12:
                                slot_ids(e + 1)
                    if k < NBLK - 1 or nxt:
                        split_x(NBLK * e + k + 1, (k + 1) % NBLK)
                    y_out(e, k)

            nc.vector.tensor_tensor_scan(flat(before[:]), flat(T["not_first"][:]), flat(T["keep"][:]), 0.0,
                                         ALU.mult, ALU.add).then_inc(prep, 1)
            dve.wait_ge(prep, 1)
            nc.vector.tensor_tensor(before[:], before[:], T["keep"][:], ALU.subtract).then_inc(marks, 1)
            for bank in (*psH, psY[BLK - 1]):
                s = nc.vector.memset(bank[:], 0.0)
            s.then_inc(cleared, 1)
            dve.wait_ge(placed, 1)
            pos = psI[0:R, 0:E * NT].rearrange("p (e t) -> p e t", e=E)
            nc.vector.tensor_copy(pos_i[:, 0], pos).then_inc(prep, 1)
            dve.wait_ge(prep, 2)
            nc.vector.tensor_scalar(pos_i[:, 1], pos_i[:, 0], 7, None, ALU.logical_shift_right).then_inc(prep, 1)
            dve.wait_ge(prep, 3)
            nc.vector.tensor_copy(T["slot_tile"][:], pos_i[:, 1])
            nc.vector.tensor_scalar(pos_i[:, 0], pos_i[:, 0], 127, None, ALU.bitwise_and).then_inc(prep, 1)
            dve.wait_ge(prep, 4)
            nc.vector.tensor_copy(before[:], pos_i[:, 0]).then_inc(prep, 1)
            dve.wait_ge(prep, 5)
            nc.vector.scalar_tensor_tensor(out=flat(before[:]), in0=flat(before[:]), scalar=1.0, in1=flat(T["keep"][:]),
                                           op0=ALU.add, op1=ALU.mult).then_inc(prep, 1)
            dve.wait_ge(prep, 6)
            nc.vector.tensor_scalar(T["slot_row"][:], before[:], -1.0, None, ALU.add).then_inc(prep, 1)
            dve.wait_ge(prep, 7)
            slot_moves(0)
            for q in range(4):
                slot_onehot(0, q)
            slot_ids(0)
            dve.wait_ge(T["w_lo_done"], PIECES * POOL_PAIRS)
            for pair in range(POOL_PAIRS, BEFORE):
                for j in range(PIECES):
                    split_pair_lo(nc.vector, T, 0, pair, j)
            split_x(0, 0)
            expert(0, True)
            with dve.Fori(1, E - 1) as e:
                expert(e, True)
            expert(E - 1, False)

        @block.tensor
        def _(pe):
            def product(out, stationary, moving, chunks, first, last):
                for c in chunks:
                    for j, (a, b) in enumerate(((0, 0), (0, 1), (1, 0))):
                        mm = nc.tensor.matmul(out, stationary(a, c), moving(b, c), start=first and c == chunks[0] and j == 0,
                                              stop=last and c == chunks[-1] and j == 2, skip_group_check=True)
                return mm

            def turn(n, k, c):
                if c == 0:
                    pe.wait_ge(gathered, 16 * BLK * (n + 1))
                if c >= 2:
                    pe.wait_ge(x_lo, DCH * n + c - 1)
                at = 0
                for t in range(BLK):
                    m = tile_rows(k, t)
                    mm = nc.tensor.transpose(psX[c % 2][:, at:at + m], xg[0:m, t, c * 128:(c + 1) * 128], T["ident"][0:m, 0:m])
                    at += m
                mm.then_inc(x_mm, 1)

            def hidden(e, k, f, n):
                if f == 0:
                    pe.wait_ge(x_lo, DCH * (NBLK * e + k + 1))
                if k == 0 and f % 2 == 0:
                    pe.wait_ge(T["w_lo_done"], PIECES * (WPAIRS * e + f // 2 + 1))
                if f >= 2 or k > 0:
                    pe.wait_ge(h_lo, STEPS * e + FCH * k + f - 1)
                product(psH[f % 2][:, 0:n], lambda a, c: w1[a][:, c, f * 128:(f + 1) * 128], lambda b, c: xT[b][:, c, 0:n],
                        range(DCH), True, True).then_inc(h_mm, 1)

            def output(e, k, f, tiles):
                pe.wait_ge(h_lo, STEPS * e + FCH * k + f + 1)
                if f == 0:
                    wait_unless_first(pe, y_done, CAPT * e + BLK * k)
                for t in range(tiles):
                    m = tile_rows(k, t)
                    mm = product(psY[t][0:m, :], lambda a, c: hT[a][:, f % 2, t * 128:t * 128 + m], lambda b, c: w2[b][:, f, :],
                                 range(1), f == 0, f == FCH - 1)
                mm.then_inc(y_mm, 1)

            def slot_product(e, q):
                pe.wait_ge(onehot_done, 4 * e + q + 1)
                if q == 0:
                    pe.wait_ge(moves_done, e + 1)
                for t in range(QUART):
                    mm = nc.tensor.matmul(psI[:, 0:CAPT * 4], onehot[:, q % 2, t, :],
                                          moves[:, q * QUART + t].rearrange("p a v -> p (a v)"),
                                          start=q == 0 and t == 0, stop=q == 3 and t == QUART - 1, skip_group_check=True)
                mm.then_inc(slot_mm, 1)

            def expert_block(e, k, nxt, tiles):
                more = k < NBLK - 1 or nxt
                n, k2 = NBLK * e + k + 1, (k + 1) % NBLK
                for f in range(FCH):
                    hidden(e, k, f, cols(k) if tiles == BLK else tiles * 128)
                    if f == FCH - 1 and more:
                        turn(n, k2, 0)
                        turn(n, k2, 1)
                    if f:
                        output(e, k, f - 1, tiles)
                    if k == 1 and nxt and f in (4, 6, 8, 10):
                        slot_product(e + 1, (f - 4) // 2)
                if more:
                    turn(n, k2, 2)
                    turn(n, k2, 3)
                output(e, k, FCH - 1, tiles)

            def expert(e, nxt):
                for k in range(NBLK):
                    full = nc.values_load(T["more"][0:1, bass.ds(e * NBLK + k, 1)], engines=(mybir.EngineType.PE,), min_val=0,
                                          max_val=1, skip_runtime_bounds_check_because="it is a comparison's result")
                    with pe.If(full == 1):
                        expert_block(e, k, nxt, BLK)
                    with pe.Else():
                        expert_block(e, k, nxt, BLK - 1)

            pe.wait_ge(marks, 1)
            nc.tensor.matmul(psI[0:R, 0:E * NT], T["after"][:], flat(T["keep"][:]), start=True, stop=False)
            nc.tensor.matmul(psI[0:R, 0:E * NT], T["ones_m"][:], flat(before[:]), start=False, stop=True).then_inc(placed, 1)
            for q in range(4):
                slot_product(0, q)
            for c in range(DCH):
                turn(0, 0, c)
            pe.wait_ge(cleared, 1)
            expert(0, True)
            with pe.Fori(1, E - 1) as e:
                expert(e, True)
            expert(E - 1, False)


def persistent(nc, ctx):
    sb = lambda name, shape, dt=F32: ctx.enter_context(nc.sbuf_tensor(name, shape, dt))
    return {
        "ident": sb("ident", [128, 128]), "ones": sb("ones", [128, 1]), "mhalf": sb("mhalf", [128, TP]), "eps": sb("eps", [128, TP]),
        "minus_one": sb("minus_one", [128, 2]),
        "flag": sb("flag", [1, 1], I32), "logits": sb("logits", [R, E, NT]),
    }


def routing(nc, ctx):
    sb = lambda name, shape, dt=F32: ctx.enter_context(nc.sbuf_tensor(name, shape, dt))
    return {
        "gate": sb("gate", [R, E, NT]), "has": sb("has", [R, E, NT]), "keep": sb("keep", [R, E, NT]),
        "gate_hi": sb("gate_hi", [R, E, NT], F32R), "vals": sb("vals", [R, E, NT, 4]),
        "slot_tile": sb("slot_tile", [R, E, NT]), "slot_row": sb("slot_row", [R, E, NT]), "not_first": sb("not_first", [R, E, NT]),
        "ones_m": sb("ones_m", [R, R]), "after": sb("after", [R, R]), "iota": sb("iota", [R, 128]),
        "iota_t": sb("iota_t", [R, CAPT]), "dump": sb("dump", [128, CAPT]),
        "more": sb("more", [1, E * NBLK], I32),
    }


def expert_weights(nc, T, ctx):
    T["w1"] = [ctx.enter_context(nc.sbuf_tensor(f"w1_{k}", [128, DCH, F], F32R)) for k in ("hi", "lo")]
    T["w2"] = [ctx.enter_context(nc.sbuf_tensor(f"w2_{k}", [128, FCH, D], F32R)) for k in ("hi", "lo")]
    T["stage"] = ctx.enter_context(nc.sbuf_tensor("stage", [128, 2, PIECES, 512], F32))
    T["w_in"] = [ctx.enter_context(nc.semaphore(f"w_in{i}")) for i in range(2)]
    T["w_hi_done"], T["w_lo_done"] = (ctx.enter_context(nc.semaphore(f"w_split_{k}")) for k in ("hi", "lo"))


def flag_value(nc, T):
    return nc.values_load(T["flag"][0:1, 0:1], min_val=0, max_val=1, skip_runtime_bounds_check_because="it is a comparison's result")


def build(nc, x, ctx, mask, wq, wk, wv, wo, bo, wr, w1, w2, out):
    A = dict(x=x.rearrange("b s d -> (b s) d"), ctx=ctx, mask=mask.bitcast(U8).rearrange("(b k) -> b k", b=B), wq=wq, wk=wk, wv=wv, wo=wo,
             bo=bo, wr=wr, w1=w1, w2=w2, out=out)
    A["xn2"] = nc.dram_tensor("xn2_rows", [NTOK, D], F32, kind="Internal").ap()
    with ExitStack() as stack:
        T = persistent(nc, stack)
        T["dump_cleared"] = stack.enter_context(nc.semaphore("dump_cleared"))
        with ExitStack() as att:
            sb = lambda name, shape, dt=F32: att.enter_context(nc.sbuf_tensor(name, shape, dt))
            T["w_hi"], T["w_lo"] = sb("w_hi", [128, WCH, D], F32R), sb("w_lo", [128, WCH, D], F32R)
            T["bias"], T["wr"] = sb("bias", [R, D]), sb("wr", [128, DCH, E])
            T["zrow"] = sb("zrow", [128, ZCOLS])
            T["x_sb"], T["c_sb"] = sb("x_sb", [R, TP, D]), sb("c_sb", [KC, TP, DC])
            T["x_in"], T["c_in"] = (att.enter_context(nc.semaphore(n)) for n in ("x_in", "c_in"))
            preamble(nc, T, A)
            with nc.If(flag_value(nc, T) == 1):
                attention_short(nc, T, A)
            with nc.Else():
                attention_general(nc, T, A)
        T |= routing(nc, stack)
        expert_weights(nc, T, stack)
        router(nc, T, A)
        with nc.If(flag_value(nc, T) == 1):
            threshold(nc, T)
        experts(nc, T, A)


_INS = ["x", "ctx_768", "mask_BxS2_bk0", "L0_xattn_W_q", "L0_xattn_W_k", "L0_xattn_W_v", "L0_xattn_W_o", "L0_xattn_b_o",
        "L0_ffn_Wr", "L0_ffn_W1", "L0_ffn_W2"]


def kernel(**inputs):
    import numpy as _np
    import concourse.bacc as _bacc
    from concourse import mybir as _mybir
    from concourse.bass_utils import run_bass_kernel_spmd as _run

    nc = _bacc.Bacc("TRN2", target_bir_lowering=False, num_devices=1)
    arrays, args = {}, []
    for name in _INS:
        a = _np.ascontiguousarray(inputs[name])
        if a.dtype == _np.bool_:
            a = a.reshape(-1).view(_np.int32)
        arrays[f"in_{name}_dram"] = a
        args.append(nc.dram_tensor(f"in_{name}_dram", a.shape, _mybir.dt.from_np(a.dtype), kind="ExternalInput").ap())
    out = nc.dram_tensor("out_0_dram", (NTOK + NDUMP, D), _mybir.dt.float32, kind="ExternalOutput").ap()
    build(nc, *args, out)
    r = _run(nc, [arrays], core_ids=[0])
    return r.results[0]["out_0_dram"][:NTOK].reshape(B, S, D)
```
